# Optimizing a Trainium2 kernel written in Bass

```python
import numpy as np
import jax
import jax.numpy as jnp

def _softmax(x, axis=-1):
    return jax.nn.softmax(x, axis=axis)

def _gelu(x):
    return jax.nn.gelu(x, approximate=True)

def _silu(x):
    return jax.nn.silu(x)

def _sigmoid(x):
    return jax.nn.sigmoid(x)

def _layernorm(x, axis=-1, eps=1e-05):
    m = jnp.mean(x, axis=axis, keepdims=True)
    v = jnp.var(x, axis=axis, keepdims=True)
    return (x - m) / jnp.sqrt(v + eps)

def _scatter_add(tgt, idx, src, axis=0):
    return tgt.at[idx].add(src)

def _segment_sum(src, seg, n):
    return jax.ops.segment_sum(src, seg, n)
kernel_name = 'mk_gnn_resnorm_d2_gnn_r32_467bbf'

def setup_inputs(seed: int=0):
    np.random.seed(seed)
    _w = jnp.asarray

    def _rec_inputs():
        import jax
        import jax.numpy as jnp
        _gk = jax.random.key(seed)
        x = -0.0001006 + 1 * jax.random.normal(jax.random.fold_in(_gk, 1), (3125, 96), jnp.float32)
        src = jax.random.randint(jax.random.fold_in(_gk, 2), (100000,), 0, 3125, jnp.int32)
        dst = jnp.minimum((3125 * jax.random.uniform(jax.random.fold_in(_gk, 3), (100000,)) ** 2.0).astype(jnp.int32), 99999)
        _o = jnp.argsort(dst, stable=True)
        src = src[_o]
        dst = dst[_o]
        return (x, src, dst)
    x, src, dst = _rec_inputs()

    def _L0_gnn_setup():
        import jax, jax.numpy as jnp
        import numpy as np
        N_NODES = 50000
        N_EDGES = 25000
        D_MODEL = 96
        HEADS = 4
        key = jax.random.key(seed)
        ks = jax.random.split(key, 6)
        scale = 1.0 / np.sqrt(D_MODEL)
        return {'embeds': jax.random.normal(ks[0], (N_NODES, D_MODEL), dtype=jnp.float32), 'qW': jax.random.normal(ks[1], (D_MODEL, D_MODEL), dtype=jnp.float32) * scale, 'kW': jax.random.normal(ks[2], (D_MODEL, D_MODEL), dtype=jnp.float32) * scale, 'vW': jax.random.normal(ks[3], (D_MODEL, D_MODEL), dtype=jnp.float32) * scale, 'rows': jax.random.randint(ks[4], (N_EDGES,), 0, N_NODES, dtype=jnp.int32), 'cols': jax.random.randint(ks[5], (N_EDGES,), 0, N_NODES, dtype=jnp.int32)}
    _L0_gnn_all = _L0_gnn_setup()
    _L0_gnn_in = {k: v for k, v in _L0_gnn_all.items() if k in ('qW', 'kW', 'vW')}
    del _L0_gnn_all

    def _L1_gnn_setup():
        import jax, jax.numpy as jnp
        import numpy as np
        N_NODES = 50000
        N_EDGES = 25000
        DIM = 96
        HEADS = 4
        LAYERS = 3
        NEG_SLOPE = 0.2

        def _gat_layer(x, src, dst, W, a_src, a_dst, b):
            N = x.shape[0]
            H, C = a_src.shape
            h = (x @ W).reshape(N, H, C)
            alpha_s = jnp.einsum('nhc,hc->nh', h, a_src)
            alpha_d = jnp.einsum('nhc,hc->nh', h, a_dst)
            e = jax.nn.leaky_relu(alpha_s[src] + alpha_d[dst], NEG_SLOPE)
            m = jax.ops.segment_max(e, dst, num_segments=N)
            m = jnp.where(jnp.isfinite(m), m, 0.0)
            ex = jnp.exp(e - m[dst])
            den = jax.ops.segment_sum(ex, dst, num_segments=N)
            alpha = ex / (den[dst] + 1e-16)
            msg = h[src] * alpha[:, :, None]
            out = jax.ops.segment_sum(msg, dst, num_segments=N)
            return out.reshape(N, H * C) + b
        key = jax.random.key(seed)
        ks = jax.random.split(key, 6)
        C = DIM // HEADS
        x = jax.random.normal(ks[0], (N_NODES, DIM), dtype=jnp.float32)
        edge_index = jax.random.randint(ks[1], (2, N_EDGES), 0, N_NODES, dtype=jnp.int32)
        W = jax.random.normal(ks[2], (LAYERS, DIM, DIM), dtype=jnp.float32) * (1.0 / np.sqrt(DIM))
        att_src = jax.random.normal(ks[3], (LAYERS, HEADS, C), dtype=jnp.float32) * (1.0 / np.sqrt(C))
        att_dst = jax.random.normal(ks[4], (LAYERS, HEADS, C), dtype=jnp.float32) * (1.0 / np.sqrt(C))
        bias = jnp.zeros((LAYERS, DIM), dtype=jnp.float32)
        return {'x': x, 'edge_index': edge_index, 'W': W, 'att_src': att_src, 'att_dst': att_dst, 'bias': bias}
    _L1_gnn_all = _L1_gnn_setup()
    _L1_gnn_in = {k: v for k, v in _L1_gnn_all.items() if k in ('W', 'att_src', 'att_dst', 'bias')}
    del _L1_gnn_all
    return {'x': x, 'src': src, 'dst': dst, 'L0_gnn_qW': _L0_gnn_in['qW'], 'L0_gnn_kW': _L0_gnn_in['kW'], 'L0_gnn_vW': _L0_gnn_in['vW'], 'L1_gnn_W': _L1_gnn_in['W'], 'L1_gnn_att_src': _L1_gnn_in['att_src'], 'L1_gnn_att_dst': _L1_gnn_in['att_dst'], 'L1_gnn_bias': _L1_gnn_in['bias']}

def reference(x, src, dst, L0_gnn_qW, L0_gnn_kW, L0_gnn_vW, L1_gnn_W, L1_gnn_att_src, L1_gnn_att_dst, L1_gnn_bias):
    import jax
    import jax.numpy as jnp

    def _L0_gnn_ref(embeds, qW, kW, vW, rows, cols):
        import jax, jax.numpy as jnp
        import numpy as np
        N_NODES = 50000
        N_EDGES = 25000
        D_MODEL = 96
        HEADS = 4
        nvar, d = embeds.shape
        dh = d // HEADS
        e = rows.shape[0]
        q = (embeds[rows] @ qW).reshape(e, HEADS, dh)
        k = (embeds[cols] @ kW).reshape(e, HEADS, dh)
        v = (embeds[cols] @ vW).reshape(e, HEADS, dh)
        scores = jnp.clip(jnp.einsum('ehd,ehd->eh', q, k), -10.0, 10.0)
        exp_s = jnp.exp(scores)
        norms = jax.ops.segment_sum(exp_s, rows, num_segments=nvar)[rows]
        w = exp_s / (norms + 1e-08)
        res = jax.ops.segment_sum(w[:, :, None] * v, rows, num_segments=nvar).reshape(nvar, d)
        return embeds + res

    def _L1_gnn_ref(x, edge_index, W, att_src, att_dst, bias):
        import jax, jax.numpy as jnp
        import numpy as np
        N_NODES = 50000
        N_EDGES = 25000
        DIM = 96
        HEADS = 4
        LAYERS = 3
        NEG_SLOPE = 0.2

        def _gat_layer(x, src, dst, W, a_src, a_dst, b):
            N = x.shape[0]
            H, C = a_src.shape
            h = (x @ W).reshape(N, H, C)
            alpha_s = jnp.einsum('nhc,hc->nh', h, a_src)
            alpha_d = jnp.einsum('nhc,hc->nh', h, a_dst)
            e = jax.nn.leaky_relu(alpha_s[src] + alpha_d[dst], NEG_SLOPE)
            m = jax.ops.segment_max(e, dst, num_segments=N)
            m = jnp.where(jnp.isfinite(m), m, 0.0)
            ex = jnp.exp(e - m[dst])
            den = jax.ops.segment_sum(ex, dst, num_segments=N)
            alpha = ex / (den[dst] + 1e-16)
            msg = h[src] * alpha[:, :, None]
            out = jax.ops.segment_sum(msg, dst, num_segments=N)
            return out.reshape(N, H * C) + b
        src = edge_index[0]
        dst = edge_index[1]
        for l in range(W.shape[0]):
            x = jax.nn.relu(_gat_layer(x, src, dst, W[l], att_src[l], att_dst[l], bias[l]))
        return x
    edge_index = jnp.stack([src, dst])
    x = _layernorm(x + _L0_gnn_ref(x, L0_gnn_qW, L0_gnn_kW, L0_gnn_vW, src, dst), axis=-1)
    x = _layernorm(x + _L1_gnn_ref(x, edge_index, L1_gnn_W, L1_gnn_att_src, L1_gnn_att_dst, L1_gnn_bias), axis=-1)
    return x

_drawn_inputs = setup_inputs


def setup_inputs(seed=0):
    import zlib

    import numpy as np

    out = dict(_drawn_inputs(seed))
    spreads = {'L1_gnn_bias': (0.0, 0.1)}
    factors = {}
    for name, (base, spread) in spreads.items():
        noise = np.random.default_rng([zlib.crc32(name.encode()), seed]).standard_normal(out[name].shape)
        drawn = base * np.exp(spread * noise) if base else spread * noise
        out[name] = jnp.asarray(drawn.astype(out[name].dtype))
    for name, factor in factors.items():
        out[name] = (out[name] * factor).astype(out[name].dtype)
    return out
```

```python
from contextlib import ExitStack

import concourse.bass as bass
from concourse import mybir

F32 = mybir.dt.float32
BF16 = mybir.dt.bfloat16
I32 = mybir.dt.int32
U32 = mybir.dt.uint32
U16 = mybir.dt.uint16
ALU = mybir.AluOpType
ACT = mybir.ActivationFunctionType
AX_X = mybir.AxisListType.X
RMAX = bass.bass_isa.ReduceOp.max

P = 128
HEADS = 4
HS = 32
PLANES = 4
RING = 5
BIG = 1.0e30
LAYERS = 3
E_LO = 4.5399929762484854e-05
E_HI = 22026.465794806718


def build(nc, x, src, dst, q_w, k_w, v_w, gat_w, att_src, att_dst, gat_b, out):
    N, D = x.shape
    E = src.shape[0]
    DH = D // HEADS
    NB = -(-N // P)
    NR = NB * P
    CH = 448
    NCH = -(-N // CH)
    NC = NCH * CH
    TG = CH // 4
    TAIL = N - (NB - 1) * P
    EP = 125
    ET = E // EP
    GROUPS = ET // PLANES
    CELLS = NR * NC
    HC = HEADS * HS + 2 * HEADS
    STEPS = NCH * NB
    ZN = CELLS // P // NC
    assert EP * ET == E and GROUPS * PLANES == ET and NB % RING == 0 and CELLS + EP < 2 ** 24

    with ExitStack() as ctx:
        def sb(name, shape, dt):
            return ctx.enter_context(nc.sbuf_tensor(name, shape, dt))

        def psum(name, shape):
            return ctx.enter_context(nc.psum_tensor(name, shape, F32))

        def sem(name):
            return ctx.enter_context(nc.semaphore(name))

        plane = [nc.dram_tensor(f"plane{i}", (CELLS + P, 1), U16).ap() for i in range(PLANES)]
        plane_v = [a[0:CELLS, :].rearrange("(b p f) o -> b p (f o)", p=P, f=NC) for a in plane]
        counts = nc.dram_tensor("counts", (NR, NR), F32).ap()

        ident = sb("ident", [P, P], F32)
        den_sel = sb("den_sel", [P, P], F32)
        zeros = sb("zeros", [P, NR], U16)
        ones = sb("ones", [P, P], F32)
        lower = sb("lower", [EP, EP], BF16)
        dump_i = sb("dump_i", [EP, 1], I32)
        dump = sb("dump", [EP, 1], F32)
        src_sb = sb("src_sb", [EP, ET], I32)
        dst_sb = sb("dst_sb", [EP, ET], I32)
        key = sb("key", [EP, ET], F32)
        keyd = sb("keyd", [EP, ET], F32)
        diag = sb("diag", [EP, 2, PLANES * EP], F32)
        same = sb("same", [EP, PLANES * EP], BF16)
        earlier = sb("earlier", [EP, PLANES * EP], BF16)
        n_earlier = sb("n_earlier", [EP, PLANES], F32)
        kfirst = sb("kfirst", [EP, PLANES], F32)
        cell = sb("cell", [EP, 4, PLANES], U32)
        addend = sb("addend", [EP, 4, PLANES], U16)

        x_sb = sb("x_sb", [P, NB, D], F32)
        w_pad = sb("w_pad", [P, 4, P], F32)
        featT = sb("featT", [P, NR], F32)
        qT = sb("qT", [P, NR], F32)
        kT = sb("kT", [P, NR], F32)
        v_sb = sb("v_sb", [P, NB, P], F32)
        resT = featT
        outT = kT
        pl_in = sb("pl_in", [P, RING, PLANES, CH], U16)
        kv_in = sb("kv_in", [P, RING, 2, P], F32)
        cnt = sb("cnt", [P, RING, CH], F32)
        wts = sb("wts", [P, RING, 2, 2 * CH], F32)
        cntT = sb("cntT", [P, RING, 4 * P], F32)
        q_c = sb("q_c", [P, CH], F32)
        num = sb("num", [P, CH], F32)
        den = sb("den", [P, CH], F32)


        x1 = qT[:].rearrange("p (b f) -> p b f", f=P)
        w_gat = sb("w_gat", [P, P], F32)
        w_gatT = sb("w_gatT", [P, P], F32)
        att_blk = sb("att_blk", [P, 2 * HEADS], F32)
        bias = sb("bias", [P, 1], F32)
        eps = sb("eps", [P, 1], F32)
        w_cat = sb("w_cat", [P, HC], F32)
        wad = sb("wad", [P, HEADS, P], F32)
        logit = sb("logit", [P, NB, 2 * HEADS], F32)
        as_in = sb("as_in", [P, RING, HEADS], F32)
        absent = sb("absent", [P, CH], F32)
        stat = sb("stat", [P, 4, NB], F32)
        h_sb, h_in, c_in = v_sb, kv_in, cnt
        flat_pl = pl_in[:].rearrange("p r q f -> p (r q f)").bitcast(F32)
        all_max = flat_pl[:, 0:HEADS * CH]
        m_row = flat_pl[:, HEADS * CH:2 * HEADS * CH]
        run_max = cntT[:].rearrange("p r f -> p (r f)")[:, 0:HEADS * CH]
        square = kT[:, 0:NB * D].rearrange("p (b f) -> p b f", f=D)

        psS = psum("psS", [P, 4, 512])
        psO = psum("psO", [P, 512])
        psP = psum("psP", [P, 2, 512])
        psD = psum("psD", [P, 512])

        G4 = [(m, g, min(4, NB - g)) for m, g in enumerate(range(0, NB, 4))]
        G3 = [(m, g, min(3, NB - g)) for m, g in enumerate(range(0, NB, 3))]
        NPREP = 2 * len(G4) + 2 * NCH
        LPREP = 2 + 2 * len(G3)
        MAXOPS = 1 + NB * (1 + HEADS)
        assert HEADS * CH <= RING * 4 * P and 2 * HEADS * CH * 4 <= RING * PLANES * CH * 2

        s_init = sem("s_init")
        s_pool0 = sem("s_pool0")
        s_edges = sem("s_edges")
        s_x = sem("s_x")
        s_zero = sem("s_zero")
        s_chain = sem("s_chain")
        s_diag = sem("s_diag")
        s_keyrow = sem("s_keyrow")
        s_dup = sem("s_dup")
        s_cell = sem("s_cell")
        s_landed = sem("s_landed")
        s_scat = [sem(f"s_scat{i}") for i in range(PLANES)]
        s_pm = sem("s_pm")
        s_pe = sem("s_pe")
        s_plane = [sem(f"s_plane{i}") for i in range(RING)]
        s_kv = [sem(f"s_kv{i}") for i in range(RING)]
        s_pair = sem("s_pair")
        s_cnt = sem("s_cnt")
        s_qc = sem("s_qc")
        s_qk = sem("s_qk")
        s_exp = sem("s_exp")
        s_clip = sem("s_clip")
        s_w = sem("s_w")
        s_pv = sem("s_pv")
        s_tr = sem("s_tr")
        s_trev = sem("s_trev")
        s_store = [sem(f"s_store{i}") for i in range(RING)]
        s_num = sem("s_num")
        s_den = sem("s_den")
        s_res = sem("s_res")
        s_ep = sem("s_ep")
        s_b1 = sem("s_b1")
        s_b1e = sem("s_b1e")
        s_x1 = sem("s_x1")
        s_b2 = sem("s_b2")
        s_b2e = sem("s_b2e")
        s_lw = sem("s_lw")
        s_lp = sem("s_lp")
        s_lpe = sem("s_lpe")
        s_wad = sem("s_wad")
        s_ad = sem("s_ad")
        s_c = [sem(f"s_c{i}") for i in range(RING)]
        s_rm = sem("s_rm")
        s_amax = sem("s_amax")
        s_m = sem("s_m")
        s_z = sem("s_z")
        s_zm = sem("s_zm")
        s_ez = sem("s_ez")
        s_gw = sem("s_gw")
        s_gpv = sem("s_gpv")
        s_relu = sem("s_relu")
        s_layer = sem("s_layer")
        s_f = sem("s_f")
        s_fe = sem("s_fe")
        s_var = sem("s_var")
        s_std = sem("s_std")
        s_stand = sem("s_stand")
        s_fin = sem("s_fin")
        s_out = sem("s_out")

        def heads(ap):
            return ap.rearrange("p (h c) -> p h c", h=HEADS)

        def stand(eng):
            eng.sem_inc(s_stand, 1)

        def one(ap):
            return ap.rearrange("p b f -> p (b f)")

        block = ctx.enter_context(nc.Block())

        @block.sync
        def _(sp):
            sp.dma_start(src_sb[:], src.rearrange("(p t) -> p t", p=EP)).then_inc(s_edges, 16)
            sp.dma_start(dst_sb[:], dst.rearrange("(p t) -> p t", p=EP)).then_inc(s_edges, 16)
            sp.wait_ge(s_init, 1)
            sp.dma_start(x_sb[:, 0:NB - 1, :], x[0:(NB - 1) * P, :].rearrange("(b p) d -> p b d", p=P)).then_inc(s_x, 16)
            sp.dma_start(x_sb[0:TAIL, NB - 1, :], x[(NB - 1) * P:N, :]).then_inc(s_x, 16)
            for j, w in enumerate((q_w, k_w, v_w)):
                sp.dma_start(heads(w_pad[0:D, j, :])[:, :, 0:DH], heads(w)).then_inc(s_x, 16)
            with sp.Fori(0, ZN) as a:
                for i in range(PLANES):
                    flat = plane[i][0:CELLS, :].rearrange("(p a f) o -> p a (f o)", p=P, a=ZN)
                    sp.dma_start(one(flat[:, bass.ds(a, 1), :]), zeros[:, 0:NC]).then_inc(s_zero, 16)
            for a in range(2):
                sp.dma_start(counts[NC:NR, a * (NR // 2):(a + 1) * (NR // 2)],
                             zeros[0:NR - NC, :].bitcast(F32)).then_inc(s_zero, 16)

            for i in range(PLANES):
                sp.wait_ge(s_scat[i], 16 * GROUPS)
            sp.wait_ge(s_pe, NPREP)
            with sp.Fori(0, NCH) as c:
                with sp.Fori(0, NB // RING) as i:
                    for j in range(RING):
                        n = c * NB + i * RING + j
                        blk = i * RING + j
                        sp.wait_ge(s_cnt, n + 1)
                        for q in range(PLANES):
                            sp.dma_start(pl_in[:, j, q, :],
                                         plane_v[q][bass.ds(blk, 1), :, bass.ds(c * CH, CH)].rearrange("b p f -> p (b f)")
                                         ).then_inc(s_plane[j], 16)
                        sp.wait_ge(s_pv, n + 1)
                        sp.dma_start(kv_in[:, j, 0, :], kT[:, bass.ds(blk * P, P)]).then_inc(s_kv[j], 16)
                        sp.dma_start(kv_in[:, j, 1, :], one(v_sb[:, bass.ds(blk, 1), :])).then_inc(s_kv[j], 16)

            for j in range(RING):
                sp.wait_ge(s_store[j], 16 * STEPS // RING + 16)
            with sp.Fori(0, LAYERS) as l:
                sp.wait_ge(s_b2e, len(G4))
                sp.wait_ge(s_layer, l + 1)
                for h in range(HEADS):
                    rows = slice(HS * h, HS * h + DH)
                    sp.dma_start(heads(w_gat[rows, :])[:, :, 0:DH],
                                 gat_w[bass.ds(l, 1), DH * h:DH * h + DH, :].rearrange("l k (h c) -> k (l h) c", h=HEADS)
                                 ).then_inc(s_lw, 16)
                    sp.dma_start(att_blk[rows, h:h + 1],
                                 att_src[bass.ds(l, 1), h:h + 1, :].rearrange("l h c -> c (l h)")).then_inc(s_lw, 16)
                    sp.dma_start(att_blk[rows, HEADS + h:HEADS + h + 1],
                                 att_dst[bass.ds(l, 1), h:h + 1, :].rearrange("l h c -> c (l h)")).then_inc(s_lw, 16)
                    sp.dma_start(bias[rows, :],
                                 gat_b[bass.ds(l, 1), DH * h:DH * h + DH].rearrange("l c -> c l")).then_inc(s_lw, 16)
                sp.wait_ge(s_lpe, (l + 1) * LPREP)
                stand(sp)

                counts_v = counts.rearrange("(b p) f -> b p f", p=P)

                def load(c, blk, j):
                    sp.dma_start(c_in[:, j, :], counts_v[bass.ds(blk, 1), :, bass.ds(c * CH, CH)]
                                 .rearrange("b p f -> p (b f)")).then_inc(s_c[j], 16)
                    sp.dma_start(h_in[:, j, 0, :], one(h_sb[:, bass.ds(blk, 1), :])).then_inc(s_c[j], 16)
                    sp.dma_start(as_in[:, j, :], one(logit[:, bass.ds(blk, 1), 0:HEADS])).then_inc(s_c[j], 16)

                with sp.Fori(0, NCH) as c:
                    t = l * NCH + c
                    sp.wait_ge(s_gpv, t * NB + RING)
                    for j in range(RING):
                        load(c, j, j)
                    with sp.Fori(1, NB // RING) as i:
                        for j in range(RING):
                            sp.wait_ge(s_rm, t * MAXOPS + 1 + (1 + HEADS) * (i * RING + j - RING + 1))
                            load(c, i * RING + j, j)
                    sp.wait_ge(s_rm, (t + 1) * MAXOPS)
                    stand(sp)
                    with sp.Fori(0, NB // RING) as i:
                        for j in range(RING):
                            sp.wait_ge(s_gpv, t * NB + i * RING + j + 1)
                            load(c, i * RING + j, j)
            sp.wait_ge(s_fin, 1)
            sp.dma_start(out[0:(NB - 1) * P, :].rearrange("(b p) d -> p b d", p=P), x_sb[:, 0:NB - 1, :]).then_inc(s_out, 16)
            sp.dma_start(out[(NB - 1) * P:N, :], x_sb[0:TAIL, NB - 1, :]).then_inc(s_out, 16)
            sp.wait_ge(s_out, 32)

        @block.gpsimd
        def _(pool):
            nc.gpsimd.memset(ones[:], 1.0).then_inc(s_pool0, 1)
            nc.gpsimd.memset(den_sel[:], 0.0).then_inc(s_pool0, 1)
            pool.wait_ge(s_pool0, 2)
            nc.gpsimd.affine_select(out=ident[:], in_=ones[:], compare_op=ALU.is_equal, fill=0.0, base=0,
                                    pattern=[[-1, P]], channel_multiplier=1).then_inc(s_pool0, 1)
            nc.gpsimd.affine_select(out=heads(den_sel[:]), in_=heads(den_sel[:]), compare_op=ALU.not_equal, fill=1.0,
                                    base=-DH, pattern=[[-HS, HEADS], [0, HS]], channel_multiplier=1).then_inc(s_pool0, 1)
            nc.gpsimd.affine_select(out=lower[:], in_=ones[0:EP, 0:EP], compare_op=ALU.is_gt, fill=0.0, base=0,
                                    pattern=[[-1, EP]], channel_multiplier=1).then_inc(s_pool0, 1)
            nc.gpsimd.iota(dump_i[:], [[0, 1]], base=CELLS, channel_multiplier=1).then_inc(s_pool0, 1)

            pool.sem_inc(s_amax, 1)
            pool.sem_inc(s_landed, 3)
            pool.wait_ge(s_zero, 16 * (ZN * PLANES + 2))

            def scatter(g, u):
                pool.wait_ge(s_cell, g + 2)
                if True:
                    for q in range(PLANES):
                        if not isinstance(g, int) or g > 0:
                            pool.wait_ge(s_scat[q], 16 * g)
                        stand(pool)
                        nc.gpsimd.indirect_dma_start(plane[q], bass.IndirectOffsetOnAxis(cell[:, u, q:q + 1], 0),
                                                     addend[:, u, q:q + 1], None, compute_op=ALU.add
                                                     ).then_inc(s_scat[q], 16)
                    pool.sem_inc(s_landed, 1)

            for u in range(4):
                scatter(u, u)
            with pool.Fori(1, GROUPS // 4) as i:
                for u in range(4):
                    scatter(i * 4 + u, u)

            with pool.Fori(0, STEPS // RING) as i:
                for j in range(RING):
                    for u in range(2):
                        pool.wait_ge(s_exp, (i * RING + j) * 2 + u + 3)
                        stand(pool)
                        nc.gpsimd.tensor_scalar(wts[:, j, u, :], wts[:, j, u, :], E_HI, E_LO, ALU.min, ALU.max
                                                ).then_inc(s_clip, 1)
            with pool.Fori(0, LAYERS * NCH) as i:
                pool.wait_ge(s_rm, (i + 1) * MAXOPS)
                stand(pool)
                nc.gpsimd.partition_all_reduce(all_max, run_max, P, RMAX).then_inc(s_amax, 1)

        @block.tensor
        def _(pe):
            pe.sem_inc(s_pv, RING)
            pe.sem_inc(s_gpv, RING)
            pe.sem_inc(s_qk, 1)
            pe.wait_ge(s_x, 80)
            pe.wait_ge(s_pool0, 6)
            m = 0

            def bank(m):
                if m >= 2:
                    pe.wait_ge(s_pe, m - 1)
                return psP[:, m % 2, :]

            for _, g, k in G4:
                ps = bank(m)
                for b in range(k):
                    last = nc.tensor.transpose(ps[0:D, b * P:(b + 1) * P], x_sb[:, g + b, :], ident[:])
                last.then_inc(s_pm, 1)
                m += 1
            pe.wait_ge(s_pe, m)
            for j in range(2):
                for c in range(NCH):
                    nc.tensor.matmul(bank(m)[:, 0:CH], w_pad[0:D, j, :], featT[0:D, c * CH:(c + 1) * CH],
                                     start=True, stop=True).then_inc(s_pm, 1)
                    m += 1
            for _, g, k in G4:
                ps = bank(m)
                for b in range(k):
                    last = nc.tensor.matmul(ps[:, b * P:(b + 1) * P], featT[0:D, (g + b) * P:(g + b + 1) * P],
                                            w_pad[0:D, 2, :], start=True, stop=True)
                last.then_inc(s_pm, 1)
                m += 1
            pe.wait_ge(s_pe, m)

            with pe.Fori(0, GROUPS // 2) as i:
                for u in range(2):
                    pe.wait_ge(s_diag, i * 2 + u + 1)
                    pe.wait_ge(s_cell, i * 2 + u + 1)
                    nc.tensor.matmul(psD[0:EP, 0:PLANES * EP], ones[0:EP, 0:EP], diag[:, u, :],
                                     start=True, stop=True).then_inc(s_keyrow, 1)

            def scores(c, j, n, k):
                pe.wait_ge(s_kv[j], 32 * (k + 1))
                for u in range(2):
                    pe.wait_ge(s_exp, 2 * n + u + 1)
                    for h in (2 * u, 2 * u + 1):
                        last = nc.tensor.matmul(psS[:, h, 0:CH], kv_in[HS * h:HS * h + HS, j, 0, :],
                                                q_c[HS * h:HS * h + HS, :], start=True, stop=True)
                    last.then_inc(s_qk, 1)

            def sums(j, n):
                pe.wait_ge(s_cnt, n + 1 + RING)
                pe.wait_ge(s_trev, n + 1)
                for g in range(4):
                    last = nc.tensor.transpose(psP[0:TG, 0, g * P:(g + 1) * P], cnt[:, j, g * TG:(g + 1) * TG], ident[:])
                last.then_inc(s_tr, 1)
                for u in range(2):
                    pe.wait_ge(s_w, 2 * n + u + 1)
                    for h in (2 * u, 2 * u + 1):
                        last = nc.tensor.matmul(psO[HS * h:HS * h + HS, 0:CH], kv_in[:, j, 1, HS * h:HS * h + HS],
                                                wts[:, j, u, (h % 2) * CH:(h % 2 + 1) * CH], start=False, stop=False,
                                                skip_group_check=True)
                last.then_inc(s_pv, 1)

            def clear_sums():
                nc.tensor.matmul(psO[:, 0:CH], zeros[:, 0:P].bitcast(BF16), zeros[:, 0:CH].bitcast(BF16),
                                 start=True, stop=False, skip_group_check=True)

            def spread_den():
                nc.tensor.matmul(psD[:, 0:CH], den_sel[:], num[:], start=True, stop=True).then_inc(s_den, 1)

            with pe.Fori(0, NCH) as c:
                pe.wait_ge(s_num, c + 1)
                pe.wait_ge(s_qc, c + 1)
                clear_sums()
                scores(c, 0, c * NB, c * (NB // RING))
                with pe.Fori(0, NB // RING - 1) as i:
                    for j in range(RING):
                        n = c * NB + i * RING + j
                        scores(c, (j + 1) % RING, n + 1, c * (NB // RING) + i + (j + 1) // RING)
                        sums(j, n)
                for j in range(RING):
                    n = c * NB + NB - RING + j
                    if j + 1 < RING:
                        scores(c, j + 1, n + 1, c * (NB // RING) + NB // RING - 1)
                    sums(j, n)
                pe.wait_ge(s_num, c + 2)
                spread_den()

            pe.wait_ge(s_res, NCH)
            pe.wait_ge(s_trev, STEPS + 1)
            for m, g, k in G4:
                if m >= 2:
                    pe.wait_ge(s_b1e, m - 1)
                for b in range(k):
                    last = nc.tensor.transpose(psP[:, m % 2, b * P:(b + 1) * P], resT[:, (g + b) * P:(g + b + 1) * P], ident[:])
                last.then_inc(s_b1, 1)
            pe.wait_ge(s_x1, 1)
            for m, g, k in G4:
                if m >= 2:
                    pe.wait_ge(s_b2e, m - 1)
                for b in range(k):
                    last = nc.tensor.transpose(psP[:, m % 2, b * P:(b + 1) * P], x1[:, g + b, :], ident[:])
                last.then_inc(s_b2, 1)
            pe.wait_ge(s_b2e, len(G4))

            with pe.Fori(0, LAYERS) as l:
                pe.wait_ge(s_layer, l + 1)
                pe.wait_ge(s_lw, (l + 1) * 16 * 4 * HEADS)
                nc.tensor.transpose(psP[:, 0, 0:P], w_gat[:], ident[:]).then_inc(s_lp, 1)
                pe.wait_ge(s_lpe, l * LPREP + 1)
                nc.tensor.matmul(psP[:, 1, 0:2 * HEADS], w_gatT[:], att_blk[:], start=True, stop=True).then_inc(s_lp, 1)
                pe.wait_ge(s_lpe, l * LPREP + 2)
                for m, g, k in G3:
                    if m >= 2:
                        pe.wait_ge(s_lpe, l * LPREP + 2 + 2 * (m - 1))
                    for b in range(k):
                        last = nc.tensor.matmul(psP[:, m % 2, b * HC:(b + 1) * HC], featT[:, (g + b) * P:(g + b + 1) * P],
                                                w_cat[:], start=True, stop=True)
                    last.then_inc(s_lp, 1)
                pe.wait_ge(s_wad, l + 1)
                stand(pe)
                with pe.Fori(0, NCH) as c:
                    t = l * NCH + c
                    pe.wait_ge(s_num, NCH + t + 1)
                    for h in range(HEADS):
                        last = nc.tensor.matmul(psS[:, h, 0:CH], wad[:, h, :], featT[:, bass.ds(c * CH, CH)],
                                                start=True, stop=True)
                    last.then_inc(s_ad, 1)
                    clear_sums()
                    with pe.Fori(0, NB // RING) as i:
                        for j in range(RING):
                            pe.wait_ge(s_gw, t * NB + i * RING + j + 1)
                            for h in range(HEADS):
                                last = nc.tensor.matmul(psO[HS * h:HS * h + HS, 0:CH], h_in[:, j, 0, HS * h:HS * h + HS],
                                                        wts[:, j, h // 2, (h % 2) * CH:(h % 2 + 1) * CH],
                                                        start=False, stop=False, skip_group_check=True)
                            last.then_inc(s_gpv, 1)
                    pe.wait_ge(s_num, NCH + t + 2)
                    spread_den()
            pe.wait_ge(s_layer, LAYERS + 1)
            for m, g, k in G4:
                if m >= 2:
                    pe.wait_ge(s_fe, m - 1)
                for b in range(k):
                    last = nc.tensor.transpose(psP[:, m % 2, b * P:(b + 1) * P], featT[:, (g + b) * P:(g + b + 1) * P], ident[:])
                last.then_inc(s_f, 1)

        @block.scalar
        def _(act):
            act.sem_inc(s_exp, 2)
            act.sem_inc(s_trev, 1)
            for j in range(RING):
                act.sem_inc(s_store[j], 16)
            act.wait_ge(s_init, 1)
            m = 0
            for _, g, k in G4:
                act.wait_ge(s_pm, m + 1)
                nc.scalar.copy(featT[0:D, g * P:(g + k) * P], psP[0:D, m % 2, 0:k * P]).then_inc(s_pe, 1)
                m += 1
            for o in (qT, kT):
                for c in range(NCH):
                    act.wait_ge(s_pm, m + 1)
                    nc.scalar.copy(o[:, c * CH:(c + 1) * CH], psP[:, m % 2, 0:CH]).then_inc(s_pe, 1)
                    m += 1
            for _, g, k in G4:
                act.wait_ge(s_pm, m + 1)
                nc.scalar.copy(v_sb[:, g:g + k, :].rearrange("p b (h c) -> p (b h) c", h=HEADS)[:, :, 0:DH],
                               psP[:, m % 2, 0:k * P].rearrange("p (a c) -> p a c", c=HS)[:, :, 0:DH]).then_inc(s_pe, 1)
                m += 1

            rows = counts[0:NC, :].rearrange("(c g p) d -> c p g d", g=4, p=TG)
            with act.Fori(0, NCH) as c:
                act.wait_ge(s_qk, 2 * NB * c + 1)
                nc.scalar.copy(q_c[:], qT[:, bass.ds(c * CH, CH)]).then_inc(s_qc, 1)
                with act.Fori(0, NB // RING) as i:
                    for j in range(RING):
                        n = c * NB + i * RING + j
                        act.wait_ge(s_pv, n + 1)
                        for u in range(2):
                            act.wait_ge(s_qk, 2 * n + u + 2)
                            nc.scalar.activation(wts[:, j, u, :].rearrange("p (v f) -> p v f", v=2),
                                                 psS[:, 2 * u:2 * u + 2, 0:CH], ACT.Exp).then_inc(s_exp, 1)
                        act.wait_ge(s_tr, n + 1)
                        act.wait_ge(s_store[j], 16 * (c * (NB // RING) + i + 1))
                        nc.scalar.copy(cntT[0:TG, j, :], psP[0:TG, 0, :]).then_inc(s_trev, 1)
                        act.wait_ge(s_trev, n + 2)
                        act.dma_start(rows[bass.ds(c, 1), :, :, bass.ds((i * RING + j) * P, P)].rearrange("c p g d -> p (c g) d"),
                                      cntT[0:TG, j, :].rearrange("p (g d) -> p g d", g=4)).then_inc(s_store[j], 16)
            act.wait_ge(s_var, 1)
            nc.scalar.activation(stat[:, 2, :], stat[:, 1, :], ACT.Sqrt, bias=eps[:], scale=1.0 / D).then_inc(s_std, 1)
            for m, g, k in G4:
                act.wait_ge(s_b2, m + 1)
                nc.scalar.copy(featT[:, g * P:(g + k) * P], psP[:, m % 2, 0:k * P]).then_inc(s_b2e, 1)

            with act.Fori(0, LAYERS) as l:
                act.wait_ge(s_lp, l * (2 + len(G3)) + 1)
                nc.scalar.copy(w_gatT[:], psP[:, 0, 0:P]).then_inc(s_lpe, 1)
                act.wait_ge(s_lw, (l + 1) * 16 * 4 * HEADS)
                nc.scalar.copy(w_cat[:, 0:P], w_gat[:])
                act.wait_ge(s_lp, l * (2 + len(G3)) + 2)
                nc.scalar.copy(w_cat[:, P:HC], psP[:, 1, 0:2 * HEADS]).then_inc(s_lpe, 1)
                for m, g, k in G3:
                    act.wait_ge(s_lp, l * (2 + len(G3)) + 3 + m)
                    ps = psP[:, m % 2, 0:k * HC].rearrange("p (b f) -> p b f", b=k)
                    nc.scalar.copy(h_sb[:, g:g + k, :].rearrange("p b (h c) -> p b h c", h=HEADS)[:, :, :, 0:DH],
                                   ps[:, :, 0:P].rearrange("p b (h c) -> p b h c", h=HEADS)[:, :, :, 0:DH]).then_inc(s_lpe, 1)
                    nc.scalar.copy(logit[:, g:g + k, :], ps[:, :, P:HC]).then_inc(s_lpe, 1)
                with act.Fori(0, NCH) as c:
                    t = l * NCH + c
                    act.wait_ge(s_ad, t + 1)
                    act.wait_ge(s_m, 4 * t + 1)
                    with act.Fori(0, NB // RING) as i:
                        for j in range(RING):
                            n = t * NB + i * RING + j
                            act.wait_ge(s_c[j], 48 * (2 * t * (NB // RING) + NB // RING + i + 1))
                            act.wait_ge(s_gpv, n + 1)
                            for h in range(HEADS):
                                last = nc.scalar.activation(wts[:, j, h // 2, (h % 2) * CH:(h % 2 + 1) * CH], psS[:, h, 0:CH],
                                                            ACT.Identity, bias=as_in[:, j, h:h + 1])
                            last.then_inc(s_z, 1)
                            act.wait_ge(s_zm, 2 * n + 2)
                            w = wts[:, j, :, :].rearrange("p u f -> p (u f)")
                            nc.scalar.activation(w, w, ACT.Exp).then_inc(s_ez, 1)
            act.wait_ge(s_var, 2)
            nc.scalar.activation(stat[:, 2, :], stat[:, 1, :], ACT.Sqrt, bias=eps[:], scale=1.0 / D).then_inc(s_std, 1)

        @block.vector
        def _(dve):
            steps = [0]

            def link(ins):
                steps[0] += 1
                ins.then_inc(s_chain, 1)
                dve.wait_ge(s_chain, steps[0])

            dve.sem_inc(s_cnt, RING)
            for s in (s_num, s_layer, s_cell):
                dve.sem_inc(s, 1)
            nc.vector.memset(x_sb[:], 0.0)
            nc.vector.memset(w_pad[:], 0.0)
            nc.vector.memset(w_gat[:], 0.0)
            nc.vector.memset(att_blk[:], 0.0)
            nc.vector.memset(bias[:], 0.0)
            nc.vector.memset(eps[:], 1e-5)
            nc.vector.memset(kT[:, NC:NR], 0.0)
            nc.vector.memset(featT[:, NC:NR], 0.0)
            nc.vector.memset(zeros[:], 0)
            link(nc.vector.memset(v_sb[:], 0.0))
            nc.vector.memset(v_sb[:].rearrange("p b (h c) -> p (b h) c", h=HEADS)[:, :, DH:DH + 1], 1.0).then_inc(s_init, 1)
            dve.wait_ge(s_edges, 32)
            dve.wait_ge(s_pool0, 6)
            link(nc.vector.tensor_copy(dump[:], dump_i[:]))
            link(nc.vector.scalar_tensor_tensor(key[:], dst_sb[:], float(NC), src_sb[:], ALU.mult, ALU.add))
            link(nc.vector.tensor_scalar(keyd[:], key[:], dump[:, 0:1], None, ALU.subtract))

            NDUP = 5
            with dve.Fori(0, GROUPS // 4) as i:
                for u in range(4):
                    g = i * 4 + u

                    def after(k):
                        dve.wait_ge(s_dup, g * NDUP + k)
                    kq = bass.ds(g * PLANES, PLANES)
                    dve.wait_ge(s_landed, g + 1)
                    nc.vector.tensor_tensor(diag[:, u % 2, :].rearrange("p (q e) -> p q e", q=PLANES),
                                            ident[0:EP, 0:EP].unsqueeze(1).to_broadcast([EP, PLANES, EP]),
                                            key[:, kq].unsqueeze(2).to_broadcast([EP, PLANES, EP]), ALU.mult).then_inc(s_diag, 1)
                    dve.wait_ge(s_keyrow, g + 1)
                    nc.vector.tensor_tensor(same[:].rearrange("p (q e) -> p q e", q=PLANES),
                                            psD[0:EP, 0:PLANES * EP].rearrange("p (q e) -> p q e", q=PLANES),
                                            key[:, kq].unsqueeze(2).to_broadcast([EP, PLANES, EP]), ALU.is_equal).then_inc(s_dup, 1)
                    after(1)
                    nc.vector.tensor_tensor(earlier[:].rearrange("p (q e) -> p q e", q=PLANES),
                                            same[:].rearrange("p (q e) -> p q e", q=PLANES),
                                            lower[:].unsqueeze(1).to_broadcast([EP, PLANES, EP]), ALU.mult).then_inc(s_dup, 1)
                    after(2)
                    nc.vector.tensor_reduce(n_earlier[:], earlier[:].rearrange("p (q e) -> p q e", q=PLANES), AX_X, ALU.add
                                            ).then_inc(s_dup, 1)
                    after(3)
                    nc.vector.scalar_tensor_tensor(kfirst[:], n_earlier[:], 0.0, keyd[:, kq], ALU.is_equal, ALU.mult).then_inc(s_dup, 1)
                    with nc.allow_low_precision("whole numbers up to 125"):
                        nc.vector.tensor_reduce(addend[:, u, :], same[:].rearrange("p (q e) -> p q e", q=PLANES), AX_X,
                                                ALU.add).then_inc(s_dup, 1)
                    after(5)
                    nc.vector.tensor_scalar(cell[:, u, :], kfirst[:], dump[:, 0:1], None, ALU.add).then_inc(s_cell, 1)

            dve.wait_ge(s_pe, len(G4))
            link(nc.vector.tensor_tensor(x_sb[:], x_sb[:], x_sb[:], ALU.add))

            def epilogue(c_now, floor, pv_done):
                dve.wait_ge(*pv_done)
                nc.vector.tensor_copy(num[:], psO[:, 0:CH]).then_inc(s_num, 1)
                dve.wait_ge(s_den, c_now + 1)
                nc.vector.tensor_scalar(den[:], psD[:, 0:CH], floor, None, ALU.add).then_inc(s_ep, 1)
                dve.wait_ge(s_ep, c_now * 3 + 1)
                nc.vector.reciprocal(den[:], den[:]).then_inc(s_ep, 1)
                dve.wait_ge(s_ep, c_now * 3 + 2)

            with dve.Fori(0, NCH) as c:
                with dve.Fori(0, NB // RING) as i:
                    for j in range(RING):
                        n = c * NB + i * RING + j
                        dve.wait_ge(s_plane[j], 16 * PLANES * (c * (NB // RING) + i + 1))
                        for q in (0, 2):
                            nc.vector.tensor_tensor(pl_in[:, j, q, :], pl_in[:, j, q, :], pl_in[:, j, q + 1, :], ALU.add
                                                    ).then_inc(s_pair, 1)
                        dve.wait_ge(s_pair, 2 * (n + 1))
                        dve.wait_ge(s_pv, n + 1)
                        nc.vector.tensor_tensor(cnt[:, j, :], pl_in[:, j, 0, :], pl_in[:, j, 2, :], ALU.add).then_inc(s_cnt, 1)
                        dve.wait_ge(s_cnt, n + 1 + RING)
                        for u in range(2):
                            dve.wait_ge(s_clip, 2 * n + u + 1)
                            w = wts[:, j, u, :].rearrange("p (v f) -> p v f", v=2)
                            nc.vector.tensor_tensor(w, w, cnt[:, j, :].unsqueeze(1).to_broadcast([P, 2, CH]), ALU.mult
                                                    ).then_inc(s_w, 1)
                epilogue(c, 1e-8, (s_pv, c * NB + NB + RING))
                nc.vector.tensor_tensor(resT[:, bass.ds(c * CH, CH)], num[:], den[:], ALU.mult).then_inc(s_ep, 1)
                dve.wait_ge(s_ep, c * 3 + 3)
                dve.sem_inc(s_res, 1)

            def layernorm(n):
                link(nc.vector.tensor_reduce(stat[:, 0, :], x_sb[:], AX_X, ALU.add))
                link(nc.vector.tensor_scalar(stat[:, 0, :], stat[:, 0, :], 1.0 / D, None, ALU.mult))
                link(nc.vector.tensor_tensor(x_sb[:], x_sb[:], stat[:, 0, :].unsqueeze(2).to_broadcast([P, NB, D]), ALU.subtract))
                link(nc.vector.tensor_tensor(square, x_sb[:], x_sb[:], ALU.mult))
                nc.vector.tensor_reduce(stat[:, 1, :], square, AX_X, ALU.add).then_inc(s_var, 1)
                dve.wait_ge(s_std, n)
                link(nc.vector.reciprocal(stat[:, 3, :], stat[:, 2, :]))

            def wide(ap):
                return ap.rearrange("p b (h c) -> p b h c", h=HEADS)[:, :, :, 0:DH]

            def narrow(ap):
                return ap.rearrange("p b (h c) -> p b h c", h=HEADS)

            for m, g, k in G4:
                dve.wait_ge(s_b1, m + 1)
                nc.vector.tensor_tensor(narrow(x_sb[:, g:g + k, :]), wide(psP[:, m % 2, 0:k * P].rearrange("p (b f) -> p b f", b=k)),
                                        narrow(x_sb[:, g:g + k, :]), ALU.add).then_inc(s_b1e, 1)
            dve.wait_ge(s_b1e, len(G4))
            link(nc.vector.memset(x1, 0.0))
            layernorm(1)
            nc.vector.tensor_tensor(wide(x1), narrow(x_sb[:]),
                                    stat[:, 3, :].unsqueeze(2).unsqueeze(3).to_broadcast([P, NB, HEADS, DH]), ALU.mult).then_inc(s_x1, 1)

            def heads_of(flat):
                return flat.rearrange("p (h f) -> p h f", h=HEADS)

            with dve.Fori(0, LAYERS) as l:
                dve.wait_ge(s_lpe, l * LPREP + 2)
                for h in range(HEADS):
                    last = nc.vector.tensor_scalar(wad[:, h, :], ones[:], w_cat[:, P + HEADS + h:P + HEADS + h + 1], None, ALU.mult)
                last.then_inc(s_wad, 1)
                with dve.Fori(0, NCH) as c:
                    t = l * NCH + c
                    dve.wait_ge(s_amax, t + 1)
                    nc.vector.memset(run_max, -2.0 * BIG).then_inc(s_rm, 1)
                    with dve.Fori(0, NB // RING) as i:
                        for j in range(RING):
                            base = t * MAXOPS + 1 + (1 + HEADS) * (i * RING + j)
                            dve.wait_ge(s_c[j], 48 * (2 * t * (NB // RING) + i + 1))
                            dve.wait_ge(s_rm, base)
                            nc.vector.tensor_scalar(absent[:], c_in[:, j, :], 0.0, -BIG, ALU.is_equal, ALU.mult).then_inc(s_rm, 1)
                            dve.wait_ge(s_rm, base + 1)
                            for h in range(HEADS):
                                r = run_max[:, h * CH:(h + 1) * CH]
                                nc.vector.scalar_tensor_tensor(r, absent[:], as_in[:, j, h:h + 1], r, ALU.add, ALU.max
                                                               ).then_inc(s_rm, 1)
                    dve.wait_ge(s_amax, t + 2)
                    dve.wait_ge(s_ad, t + 1)
                    nc.vector.tensor_tensor(heads_of(m_row), psS[:, :, 0:CH], heads_of(all_max), ALU.add).then_inc(s_m, 1)
                    dve.wait_ge(s_m, 4 * t + 1)
                    nc.vector.scalar_tensor_tensor(m_row, m_row, 0.2, m_row, ALU.mult, ALU.max).then_inc(s_m, 1)
                    nc.vector.tensor_scalar(all_max, all_max, -0.5 * BIG, None, ALU.is_gt).then_inc(s_m, 1)
                    dve.wait_ge(s_m, 4 * t + 3)
                    nc.vector.tensor_tensor(m_row, m_row, all_max, ALU.mult).then_inc(s_m, 1)
                    dve.wait_ge(s_m, 4 * t + 4)
                    stand(dve)
                    with dve.Fori(0, NB // RING) as i:
                        for j in range(RING):
                            n = t * NB + i * RING + j
                            w = wts[:, j, :, :].rearrange("p u f -> p (u f)")
                            dve.wait_ge(s_z, n + 1)
                            nc.vector.scalar_tensor_tensor(w, w, 0.2, w, ALU.mult, ALU.max).then_inc(s_zm, 1)
                            dve.wait_ge(s_zm, 2 * n + 1)
                            nc.vector.tensor_tensor(w, w, m_row, ALU.subtract).then_inc(s_zm, 1)
                            dve.wait_ge(s_ez, n + 1)
                            dve.wait_ge(s_c[j], 48 * (2 * t * (NB // RING) + NB // RING + i + 1))
                            nc.vector.scalar_tensor_tensor(heads_of(w), heads_of(w), 1.0,
                                                           c_in[:, j, :].unsqueeze(1).to_broadcast([P, HEADS, CH]),
                                                           ALU.min, ALU.mult).then_inc(s_gw, 1)
                    epilogue(NCH + t, 1e-16, (s_gpv, t * NB + NB + RING))
                    o = outT[:, bass.ds(c * CH, CH)]
                    nc.vector.tensor_tensor(num[:], num[:], den[:], ALU.mult).then_inc(s_ep, 1)
                    dve.wait_ge(s_ep, (NCH + t) * 3 + 3)
                    nc.vector.tensor_scalar(o, num[:], bias[:, 0:1], 0.0, ALU.add, ALU.max).then_inc(s_relu, 1)
                dve.wait_ge(s_relu, (l + 1) * NCH)
                nc.vector.tensor_copy(featT[:, 0:NC], outT[:, 0:NC]).then_inc(s_layer, 1)

            for m, g, k in G4:
                dve.wait_ge(s_f, m + 1)
                nc.vector.tensor_tensor(narrow(x_sb[:, g:g + k, :]), wide(psP[:, m % 2, 0:k * P].rearrange("p (b f) -> p b f", b=k)),
                                        wide(x1[:, g:g + k, :]), ALU.add).then_inc(s_fe, 1)
            dve.wait_ge(s_fe, len(G4))
            layernorm(2)
            nc.vector.tensor_tensor(x_sb[:], x_sb[:], stat[:, 3, :].unsqueeze(2).to_broadcast([P, NB, D]), ALU.mult).then_inc(s_fin, 1)


_INS = ["x", "src", "dst", "L0_gnn_qW", "L0_gnn_kW", "L0_gnn_vW", "L1_gnn_W", "L1_gnn_att_src", "L1_gnn_att_dst", "L1_gnn_bias"]


def kernel(**inputs):
    import numpy as _np
    import concourse.bacc as _bacc
    from concourse import mybir as _mybir
    from concourse.bass_utils import run_bass_kernel_spmd as _run

    nc = _bacc.Bacc("TRN2", target_bir_lowering=False, num_devices=1)
    arrays, args = {}, []
    for name in _INS:
        a = _np.ascontiguousarray(inputs[name])
        arrays[f"in_{name}_dram"] = a
        args.append(nc.dram_tensor(f"in_{name}_dram", a.shape, _mybir.dt.from_np(a.dtype), kind="ExternalInput").ap())
    x = inputs["x"]
    args.append(nc.dram_tensor("out_0_dram", x.shape, _mybir.dt.float32, kind="ExternalOutput").ap())
    build(nc, *args)
    r = _run(nc, [arrays], core_ids=[0])
    return r.results[0]["out_0_dram"]
```

```python
from contextlib import ExitStack

import concourse.bass as bass
from concourse import mybir

F32 = mybir.dt.float32
BF16 = mybir.dt.bfloat16
I32 = mybir.dt.int32
U32 = mybir.dt.uint32
U16 = mybir.dt.uint16
ALU = mybir.AluOpType
ACT = mybir.ActivationFunctionType
AX_X = mybir.AxisListType.X
RMAX = bass.bass_isa.ReduceOp.max

P = 128
HEADS = 4
HS = 32
PLANES = 4
RING = 5
BIG = 1.0e30
LAYERS = 3
SPREAD = 60.0
COUNT = 256.0
OWN = 7
E_LO = 4.5399929762484854e-05
E_HI = 22026.465794806718


def build(nc, x, src, dst, q_w, k_w, v_w, gat_w, att_src, att_dst, gat_b, out):
    N, D = x.shape
    E = src.shape[0]
    DH = D // HEADS
    NB = -(-N // P)
    NR = NB * P
    CH = 448
    NCH = -(-N // CH)
    NC = NCH * CH
    TG = CH // 4
    TAIL = N - (NB - 1) * P
    EP = 125
    ET = E // EP
    GROUPS = ET // PLANES
    CELLS = NR * NC
    HC = HEADS * HS + 2 * HEADS
    STEPS = NCH * NB
    FB = 5
    FC = FB * P
    NFC = NB // FB
    AW = 400
    ZN = CELLS // P // NC
    assert EP * ET == E and GROUPS * PLANES == ET and NB % RING == 0 and CELLS + EP < 2 ** 24

    with ExitStack() as ctx:
        def sb(name, shape, dt, span=ctx):
            return span.enter_context(nc.sbuf_tensor(name, shape, dt))

        def stage():
            return ExitStack()

        def psum(name, shape):
            return ctx.enter_context(nc.psum_tensor(name, shape, F32))

        def sem(name):
            return ctx.enter_context(nc.semaphore(name))

        plane = [nc.dram_tensor(f"plane{i}", (CELLS + P, 1), U16).ap() for i in range(PLANES)]
        plane_v = [a[0:CELLS, :].rearrange("(b p f) o -> b p (f o)", p=P, f=NC) for a in plane]
        counts = nc.dram_tensor("counts", (NR, NR), F32).ap()
        counts16 = nc.dram_tensor("counts16", (NR, NR), BF16).ap()

        ident = sb("ident", [P, P], F32)
        den_sel = sb("den_sel", [P, P], F32)
        ones = sb("ones", [P, P], F32)
        zero16 = sb("zero16", [P, 512], BF16)
        featT = sb("featT", [P, NR], F32)
        resT = featT
        qT = sb("qT", [P, NR], F32)
        kT = sb("kT", [P, NR], F32)
        v_sb = sb("v_sb", [P, NB, P], F32)
        h_sb = v_sb
        x1 = qT[:].rearrange("p (b f) -> p b f", f=P)
        outT = kT
        square = kT[:, 0:NB * D].rearrange("p (b f) -> p b f", f=D)
        w_gat = sb("w_gat", [P, P], F32)
        w_gatT = sb("w_gatT", [P, P], F32)
        att_blk = sb("att_blk", [P, 2 * HEADS], F32)
        bias = sb("bias", [P, 1], F32)
        bias_row = sb("bias_row", [P, D], F32)
        eps = sb("eps", [P, 1], F32)
        w_cat = sb("w_cat", [P, HC], F32)
        wad = sb("wad", [P, HEADS, P], F32)
        logit = sb("logit", [P, NB, 2 * HEADS], F32)
        stat = sb("stat", [P, 4, NB], F32)
        step_max = sb("step_max", [P, RING], F32)
        extreme = sb("extreme", [P, 2 * HEADS + 1], F32)
        extremes = sb("extremes", [P, 2 * HEADS + 1], F32)
        spread = sb("spread", [P, HEADS + 2], F32)
        route_f = sb("route_f", [1, 3], F32)
        route = sb("route", [1, 3], I32)

        with stage() as span:
            x_sb = sb("x_sb", [P, NB, D], F32, span)
            w_pad = sb("w_pad", [P, 4, P], F32, span)
            zeros = sb("zeros", [P, NR], U16, span)
            lower = sb("lower", [EP, EP], BF16, span)
            dump_i = sb("dump_i", [EP, 1], I32, span)
            dump = sb("dump", [EP, 1], F32, span)
            src_sb = sb("src_sb", [EP, ET], I32, span)
            dst_sb = sb("dst_sb", [EP, ET], I32, span)
            key = sb("key", [EP, ET], F32, span)
            keyd = sb("keyd", [EP, ET], F32, span)
            diag = sb("diag", [EP, 2, PLANES * EP], F32, span)
            same = sb("same", [EP, PLANES * EP], BF16, span)
            earlier = sb("earlier", [EP, PLANES * EP], BF16, span)
            n_earlier = sb("n_earlier", [EP, PLANES], F32, span)
            kfirst = sb("kfirst", [EP, PLANES], F32, span)
            cell = sb("cell", [EP, 4, PLANES], U32, span)
            addend = sb("addend", [EP, 4, PLANES], U16, span)
            pl_in = sb("pl_in", [P, RING, PLANES, CH], U16, span)
            kv_in = sb("kv_in", [P, RING, 2, P], F32, span)
            cnt = sb("cnt", [P, RING, CH], F32, span)
            cntT = sb("cntT", [P, RING, 4 * P], F32, span)
            cntT16 = sb("cntT16", [P, RING, 4 * P], BF16, span)
            q_c = sb("q_c", [P, CH], F32, span)
            num = sb("num", [P, CH], F32, span)
            den = sb("den", [P, CH], F32, span)
            wts = sb("wts", [P, RING, 2, 2 * CH], F32, span)

        with stage() as span:
            g_hold = sb("g_hold", [P, NB * P], F32, span)
            h_in = sb("h_in", [P, RING, P], F32, span)
            c_in = sb("c_in", [P, RING, CH], F32, span)
            as_in = sb("as_in", [P, RING, HEADS], F32, span)
            g_wts = sb("g_wts", [P, RING, HEADS * CH], F32, span)
            g_num = sb("g_num", [P, CH], F32, span)
            g_den = sb("g_den", [P, CH], F32, span)
            absent = sb("absent", [P, CH], F32, span)
            run_max = sb("run_max", [P, HEADS * CH], F32, span)[:]
            all_max = sb("all_max", [P, HEADS * CH], F32, span)[:]
            m_row = sb("m_row", [P, HEADS * CH], F32, span)[:]

        with stage() as span:
            room = sb("room", [P, NB * HEADS * 2 * (DH + 1)], F32, span)
            terms = room[:].rearrange("p (a f) -> p a f", f=2 * (DH + 1))
            sums = room[:, 0:FB * 500].rearrange("p (d f) -> p d f", d=FB)
            x_next = room[:, 0:NB * P].rearrange("p (b f) -> p b f", f=P)
            y_sb = room[:, 0:NB * D].rearrange("p (b f) -> p b f", f=D)
            parts = sb("parts", [P, NB * HEADS, 3, 2 * (DH + 1)], BF16, span)
            neg_as = sb("neg_as", [P, NB, HEADS], F32, span)
            scale_s = sb("scale_s", [P, NB, HEADS, 2], F32, span)
            scale_d = sb("scale_d", [P, 2, NB, HEADS], F32, span)
            ad_row = sb("ad_row", [P, HEADS, NR], F32, span)
            c16 = sb("c16", [P, RING, FC], BF16, span)
            chosen = sb("chosen", [P, 10, FC], BF16, span)
            rden = sb("rden", [P, NB, HEADS], F32, span)
            total = outT[:, 0:NB * HEADS * (DH + 1)].rearrange("p (b h f) -> p b h f", h=HEADS, f=DH + 1)

        acc = psum("acc", [P, 8, 512])
        psS = acc[:, 0:4]
        psO = acc[:, 4]
        psP = acc[:, 5:7]
        psD = acc[:, 7]

        G4 = [(m, g, min(4, NB - g)) for m, g in enumerate(range(0, NB, 4))]
        G3 = [(m, g, min(3, NB - g)) for m, g in enumerate(range(0, NB, 3))]
        NPREP = 2 * len(G4) + 2 * NCH
        LPREP = 2 + 2 * len(G3)
        MAXOPS = 1 + NB * (1 + HEADS)

        s_init = sem("s_init")
        s_pool0 = sem("s_pool0")
        s_edges = sem("s_edges")
        s_x = sem("s_x")
        s_zero = sem("s_zero")
        s_chain = sem("s_chain")
        s_diag = sem("s_diag")
        s_keyrow = sem("s_keyrow")
        s_dup = sem("s_dup")
        s_cell = sem("s_cell")
        s_landed = sem("s_landed")
        s_scat = [sem(f"s_scat{i}") for i in range(PLANES)]
        s_pm = sem("s_pm")
        s_pe = sem("s_pe")
        s_plane = [sem(f"s_plane{i}") for i in range(RING)]
        s_kv = [sem(f"s_kv{i}") for i in range(RING)]
        s_pair = sem("s_pair")
        s_cnt = sem("s_cnt")
        s_qc = sem("s_qc")
        s_qk = sem("s_qk")
        s_exp = sem("s_exp")
        s_clip = sem("s_clip")
        s_w = sem("s_w")
        s_pv = sem("s_pv")
        s_tr = sem("s_tr")
        s_trev = sem("s_trev")
        s_store = [sem(f"s_store{i}") for i in range(RING)]
        s_num = sem("s_num")
        s_den = sem("s_den")
        s_res = sem("s_res")
        s_ep = sem("s_ep")
        s_b1 = sem("s_b1")
        s_b1e = sem("s_b1e")
        s_x1 = sem("s_x1")
        s_b2 = sem("s_b2")
        s_b2e = sem("s_b2e")
        s_lw = sem("s_lw")
        s_lp = sem("s_lp")
        s_lpe = sem("s_lpe")
        s_wad = sem("s_wad")
        s_ad = sem("s_ad")
        s_c = [sem(f"s_c{i}") for i in range(RING)]
        s_rm = sem("s_rm")
        s_amax = sem("s_amax")
        s_m = sem("s_m")
        s_z = sem("s_z")
        s_zm = sem("s_zm")
        s_ez = sem("s_ez")
        s_gw = sem("s_gw")
        s_gpv = sem("s_gpv")
        s_relu = sem("s_relu")
        s_layer = sem("s_layer")
        s_f = sem("s_f")
        s_fe = sem("s_fe")
        s_var = sem("s_var")
        s_std = sem("s_std")
        s_lay = sem("s_lay")
        s_lay2 = sem("s_lay2")
        s_own = sem("s_own")
        s_route = sem("s_route")
        s_ext = sem("s_ext")
        s_ar = sem("s_ar")
        s_sc = sem("s_sc")
        s_sce = sem("s_sce")
        s_term = sem("s_term")
        s_part = sem("s_part")
        s_low = sem("s_low")
        s_adr = sem("s_adr")
        s_adre = sem("s_adre")
        s_fc = [sem(f"s_fc{i}") for i in range(RING)]
        s_chosen = sem("s_chosen")
        s_head = sem("s_head")
        s_fsum = sem("s_fsum")
        s_comb = sem("s_comb")
        s_xn = sem("s_xn")
        s_xt = sem("s_xt")
        s_xte = sem("s_xte")
        s_stand = sem("s_stand")
        s_fin = sem("s_fin")
        s_out = sem("s_out")

        def heads(ap):
            return ap.rearrange("p (h c) -> p h c", h=HEADS)

        def stand(eng):
            eng.sem_inc(s_stand, 1)

        def one(ap):
            return ap.rearrange("p b f -> p (b f)")

        block = ctx.enter_context(nc.Block())

        @block.sync
        def _(sp):
            sp.dma_start(src_sb[:], src.rearrange("(p t) -> p t", p=EP)).then_inc(s_edges, 16)
            sp.dma_start(dst_sb[:], dst.rearrange("(p t) -> p t", p=EP)).then_inc(s_edges, 16)
            sp.wait_ge(s_init, 1)
            sp.dma_start(x_sb[:, 0:NB - 1, :], x[0:(NB - 1) * P, :].rearrange("(b p) d -> p b d", p=P)).then_inc(s_x, 16)
            sp.dma_start(x_sb[0:TAIL, NB - 1, :], x[(NB - 1) * P:N, :]).then_inc(s_x, 16)
            for j, w in enumerate((q_w, k_w, v_w)):
                sp.dma_start(heads(w_pad[0:D, j, :])[:, :, 0:DH], heads(w)).then_inc(s_x, 16)
            with sp.Fori(0, ZN) as a:
                for i in range(PLANES):
                    flat = plane[i][0:CELLS, :].rearrange("(p a f) o -> p a (f o)", p=P, a=ZN)
                    sp.dma_start(one(flat[:, bass.ds(a, 1), :]), zeros[:, 0:NC]).then_inc(s_zero, 16)
            for a in range(2):
                sp.dma_start(counts[NC:NR, a * (NR // 2):(a + 1) * (NR // 2)],
                             zeros[0:NR - NC, :].bitcast(F32)).then_inc(s_zero, 16)
            sp.dma_start(counts16[NC:NR, :], zeros[0:NR - NC, :].bitcast(BF16)).then_inc(s_zero, 16)

            for i in range(PLANES):
                sp.wait_ge(s_scat[i], 16 * GROUPS)
            sp.wait_ge(s_pe, NPREP)
            with sp.Fori(0, NCH) as c:
                with sp.Fori(0, NB // RING) as i:
                    for j in range(RING):
                        n = c * NB + i * RING + j
                        blk = i * RING + j
                        sp.wait_ge(s_cnt, n + 1)
                        for q in range(PLANES):
                            sp.dma_start(pl_in[:, j, q, :],
                                         plane_v[q][bass.ds(blk, 1), :, bass.ds(c * CH, CH)].rearrange("b p f -> p (b f)")
                                         ).then_inc(s_plane[j], 16)
                        sp.wait_ge(s_pv, n + 1)
                        sp.dma_start(kv_in[:, j, 0, :], kT[:, bass.ds(blk * P, P)]).then_inc(s_kv[j], 16)
                        sp.dma_start(kv_in[:, j, 1, :], one(v_sb[:, bass.ds(blk, 1), :])).then_inc(s_kv[j], 16)

            for j in range(RING):
                sp.wait_ge(s_store[j], 32 * STEPS // RING + 32)
            with sp.Fori(0, LAYERS) as l:
                sp.wait_ge(s_b2e, len(G4))
                sp.wait_ge(s_layer, l + 1)
                for h in range(HEADS):
                    rows = slice(HS * h, HS * h + DH)
                    sp.dma_start(heads(w_gat[rows, :])[:, :, 0:DH],
                                 gat_w[bass.ds(l, 1), DH * h:DH * h + DH, :].rearrange("l k (h c) -> k (l h) c", h=HEADS)
                                 ).then_inc(s_lw, 16)
                    sp.dma_start(att_blk[rows, h:h + 1],
                                 att_src[bass.ds(l, 1), h:h + 1, :].rearrange("l h c -> c (l h)")).then_inc(s_lw, 16)
                    sp.dma_start(att_blk[rows, HEADS + h:HEADS + h + 1],
                                 att_dst[bass.ds(l, 1), h:h + 1, :].rearrange("l h c -> c (l h)")).then_inc(s_lw, 16)
                    sp.dma_start(bias[rows, :],
                                 gat_b[bass.ds(l, 1), DH * h:DH * h + DH].rearrange("l c -> c l")).then_inc(s_lw, 16)
                sp.dma_start(bias_row[:], gat_b[bass.ds(l, 1), :].partition_broadcast(P).rearrange("p l c -> p (l c)")).then_inc(s_lw, 16)

                sp.wait_ge(s_route, l + 1)
                stand(sp)
                general = sp.value_load(route[0:1, 0:1], min_val=0, max_val=1)
                g = sp.value_load(route[0:1, 1:2], min_val=0, max_val=LAYERS)
                f = sp.value_load(route[0:1, 2:3], min_val=0, max_val=LAYERS)
                with sp.If(general == 1):
                    counts_v = counts.rearrange("(b p) f -> b p f", p=P)

                    def load(c, blk, j):
                        sp.dma_start(c_in[:, j, :], counts_v[bass.ds(blk, 1), :, bass.ds(c * CH, CH)]
                                     .rearrange("b p f -> p (b f)")).then_inc(s_c[j], 16)
                        sp.dma_start(h_in[:, j, :], one(h_sb[:, bass.ds(blk, 1), :])).then_inc(s_c[j], 16)
                        sp.dma_start(as_in[:, j, :], one(logit[:, bass.ds(blk, 1), 0:HEADS])).then_inc(s_c[j], 16)

                    with sp.Fori(0, NCH) as c:
                        t = g * NCH + c
                        sp.wait_ge(s_gpv, t * NB + RING)
                        for j in range(RING):
                            load(c, j, j)
                        with sp.Fori(1, NB // RING) as i:
                            for j in range(RING):
                                sp.wait_ge(s_rm, t * MAXOPS + 1 + (1 + HEADS) * (i * RING + j - RING + 1))
                                load(c, i * RING + j, j)
                        sp.wait_ge(s_rm, (t + 1) * MAXOPS)
                        stand(sp)
                        with sp.Fori(0, NB // RING) as i:
                            for j in range(RING):
                                sp.wait_ge(s_gpv, t * NB + i * RING + j + 1)
                                load(c, i * RING + j, j)
                with sp.Else():
                    counts16_v = counts16.rearrange("(b p) f -> b p f", p=P)
                    with sp.Fori(0, NFC) as c:
                        with sp.Fori(0, NFC) as i:
                            for j in range(RING):
                                n = (f * NFC + c) * NB + i * RING + j
                                sp.wait_ge(s_head, HEADS * n + HEADS)
                                sp.dma_start(c16[:, j, :], counts16_v[bass.ds(i * RING + j, 1), :, bass.ds(c * FC, FC)]
                                             .rearrange("b p f -> p (b f)")).then_inc(s_fc[j], 16)
            sp.wait_ge(s_fin, 1)
            sp.dma_start(out[0:(NB - 1) * P, :].rearrange("(b p) d -> p b d", p=P), y_sb[:, 0:NB - 1, :]).then_inc(s_out, 16)
            sp.dma_start(out[(NB - 1) * P:N, :], y_sb[0:TAIL, NB - 1, :]).then_inc(s_out, 16)
            sp.wait_ge(s_out, 32)

        @block.gpsimd
        def _(pool):
            nc.gpsimd.memset(ones[:], 1.0).then_inc(s_pool0, 1)
            nc.gpsimd.memset(den_sel[:], 0.0).then_inc(s_pool0, 1)
            pool.wait_ge(s_pool0, 2)
            nc.gpsimd.affine_select(out=ident[:], in_=ones[:], compare_op=ALU.is_equal, fill=0.0, base=0,
                                    pattern=[[-1, P]], channel_multiplier=1).then_inc(s_pool0, 1)
            nc.gpsimd.affine_select(out=heads(den_sel[:]), in_=heads(den_sel[:]), compare_op=ALU.not_equal, fill=1.0,
                                    base=-DH, pattern=[[-HS, HEADS], [0, HS]], channel_multiplier=1).then_inc(s_pool0, 1)
            nc.gpsimd.affine_select(out=lower[:], in_=ones[0:EP, 0:EP], compare_op=ALU.is_gt, fill=0.0, base=0,
                                    pattern=[[-1, EP]], channel_multiplier=1).then_inc(s_pool0, 1)
            nc.gpsimd.iota(dump_i[:], [[0, 1]], base=CELLS, channel_multiplier=1).then_inc(s_pool0, 1)

            pool.sem_inc(s_amax, 1)
            pool.sem_inc(s_comb, 1)
            pool.sem_inc(s_landed, 3)
            pool.wait_ge(s_zero, 16 * (ZN * PLANES + 3))

            def scatter(g, u):
                pool.wait_ge(s_cell, g + 2)
                if True:
                    for q in range(PLANES):
                        if not isinstance(g, int) or g > 0:
                            pool.wait_ge(s_scat[q], 16 * g)
                        stand(pool)
                        nc.gpsimd.indirect_dma_start(plane[q], bass.IndirectOffsetOnAxis(cell[:, u, q:q + 1], 0),
                                                     addend[:, u, q:q + 1], None, compute_op=ALU.add
                                                     ).then_inc(s_scat[q], 16)
                    pool.sem_inc(s_landed, 1)

            for u in range(4):
                scatter(u, u)
            with pool.Fori(1, GROUPS // 4) as i:
                for u in range(4):
                    scatter(i * 4 + u, u)

            with pool.Fori(0, STEPS // RING) as i:
                for j in range(RING):
                    for u in range(2):
                        pool.wait_ge(s_exp, (i * RING + j) * 2 + u + 3)
                        stand(pool)
                        nc.gpsimd.tensor_scalar(wts[:, j, u, :], wts[:, j, u, :], E_HI, E_LO, ALU.min, ALU.max
                                                ).then_inc(s_clip, 1)
            with pool.Fori(0, LAYERS) as l:
                pool.wait_ge(s_ext, l + 1)
                stand(pool)
                nc.gpsimd.partition_all_reduce(extremes[:], extreme[:], P, RMAX).then_inc(s_ar, 1)
                pool.wait_ge(s_route, l + 1)
                stand(pool)
                general = pool.value_load(route[0:1, 0:1], min_val=0, max_val=1)
                g = pool.value_load(route[0:1, 1:2], min_val=0, max_val=LAYERS)
                f = pool.value_load(route[0:1, 2:3], min_val=0, max_val=LAYERS)
                with pool.If(general == 1):
                    with pool.Fori(0, NCH) as c:
                        pool.wait_ge(s_rm, (g * NCH + c + 1) * MAXOPS)
                        stand(pool)
                        nc.gpsimd.partition_all_reduce(all_max, run_max, P, RMAX).then_inc(s_amax, 1)
                with pool.Else():
                    with pool.Fori(0, NFC) as c:
                        t = f * NFC + c
                        pool.wait_ge(s_fsum, (t + 1) * FB + 1)

                        def after(k):
                            pool.wait_ge(s_comb, 4 * t + k + 1)
                            stand(pool)
                        W = DH + 1
                        s4 = sums[:, :, 0:HEADS * 4 * W].rearrange("p d (h f) -> p d h f", h=HEADS)
                        both = s4[:, :, :, 0:2 * W]
                        stand(pool)
                        nc.gpsimd.tensor_tensor(both, both, s4[:, :, :, 2 * W:4 * W], ALU.add).then_inc(s_comb, 1)
                        after(1)
                        low = s4[:, :, :, W:2 * W]
                        nc.gpsimd.tensor_tensor(low, sums[:, :, HEADS * 4 * W:HEADS * 5 * W].rearrange("p d (h f) -> p d h f", h=HEADS),
                                                low, ALU.subtract).then_inc(s_comb, 1)
                        after(2)
                        for k in range(2):
                            v = s4[:, :, :, k * W:(k + 1) * W]
                            last = nc.gpsimd.tensor_tensor(v, v, scale_d[:, k, bass.ds(c * FB, FB), :].unsqueeze(3)
                                                           .to_broadcast([P, FB, HEADS, W]), ALU.mult)
                        last.then_inc(s_comb, 1)
                        after(3)
                        nc.gpsimd.tensor_tensor(total[:, bass.ds(c * FB, FB), :, :], s4[:, :, :, 0:W], low, ALU.add).then_inc(s_comb, 1)

        @block.tensor
        def _(pe):
            pe.sem_inc(s_pv, RING)
            pe.sem_inc(s_gpv, RING)
            pe.sem_inc(s_head, HEADS * RING)
            pe.sem_inc(s_qk, 1)
            pe.wait_ge(s_x, 80)
            pe.wait_ge(s_pool0, 6)
            m = 0

            def bank(m):
                if m >= 2:
                    pe.wait_ge(s_pe, m - 1)
                return psP[:, m % 2, :]

            for _, g, k in G4:
                ps = bank(m)
                for b in range(k):
                    last = nc.tensor.transpose(ps[0:D, b * P:(b + 1) * P], x_sb[:, g + b, :], ident[:])
                last.then_inc(s_pm, 1)
                m += 1
            pe.wait_ge(s_pe, m)
            for j in range(2):
                for c in range(NCH):
                    nc.tensor.matmul(bank(m)[:, 0:CH], w_pad[0:D, j, :], featT[0:D, c * CH:(c + 1) * CH],
                                     start=True, stop=True).then_inc(s_pm, 1)
                    m += 1
            for _, g, k in G4:
                ps = bank(m)
                for b in range(k):
                    last = nc.tensor.matmul(ps[:, b * P:(b + 1) * P], featT[0:D, (g + b) * P:(g + b + 1) * P],
                                            w_pad[0:D, 2, :], start=True, stop=True)
                last.then_inc(s_pm, 1)
                m += 1
            pe.wait_ge(s_pe, m)

            with pe.Fori(0, GROUPS // 2) as i:
                for u in range(2):
                    pe.wait_ge(s_diag, i * 2 + u + 1)
                    pe.wait_ge(s_cell, i * 2 + u + 1)
                    nc.tensor.matmul(psD[0:EP, 0:PLANES * EP], ones[0:EP, 0:EP], diag[:, u, :],
                                     start=True, stop=True).then_inc(s_keyrow, 1)

            def scores(c, j, n, k):
                pe.wait_ge(s_kv[j], 32 * (k + 1))
                for u in range(2):
                    pe.wait_ge(s_exp, 2 * n + u + 1)
                    for h in (2 * u, 2 * u + 1):
                        last = nc.tensor.matmul(psS[:, h, 0:CH], kv_in[HS * h:HS * h + HS, j, 0, :],
                                                q_c[HS * h:HS * h + HS, :], start=True, stop=True)
                    last.then_inc(s_qk, 1)

            def sums(j, n):
                pe.wait_ge(s_cnt, n + 1 + RING)
                pe.wait_ge(s_trev, 2 * n + 1)
                for g in range(4):
                    last = nc.tensor.transpose(psP[0:TG, 0, g * P:(g + 1) * P], cnt[:, j, g * TG:(g + 1) * TG], ident[:])
                last.then_inc(s_tr, 1)
                for u in range(2):
                    pe.wait_ge(s_w, 2 * n + u + 1)
                    for h in (2 * u, 2 * u + 1):
                        last = nc.tensor.matmul(psO[HS * h:HS * h + HS, 0:CH], kv_in[:, j, 1, HS * h:HS * h + HS],
                                                wts[:, j, u, (h % 2) * CH:(h % 2 + 1) * CH], start=False, stop=False,
                                                skip_group_check=True)
                last.then_inc(s_pv, 1)

            def clear_sums():
                nc.tensor.matmul(psO[:, 0:CH], zero16[:, 0:P], zero16[:, 0:CH],
                                 start=True, stop=False, skip_group_check=True)

            def spread_den():
                nc.tensor.matmul(psD[:, 0:CH], den_sel[:], num[:], start=True, stop=True).then_inc(s_den, 1)

            with pe.Fori(0, NCH) as c:
                pe.wait_ge(s_num, c + 1)
                pe.wait_ge(s_qc, c + 1)
                clear_sums()
                scores(c, 0, c * NB, c * (NB // RING))
                with pe.Fori(0, NB // RING - 1) as i:
                    for j in range(RING):
                        n = c * NB + i * RING + j
                        scores(c, (j + 1) % RING, n + 1, c * (NB // RING) + i + (j + 1) // RING)
                        sums(j, n)
                for j in range(RING):
                    n = c * NB + NB - RING + j
                    if j + 1 < RING:
                        scores(c, j + 1, n + 1, c * (NB // RING) + NB // RING - 1)
                    sums(j, n)
                pe.wait_ge(s_num, c + 2)
                spread_den()

            pe.wait_ge(s_res, NCH)
            pe.wait_ge(s_trev, 2 * STEPS + 1)
            for m, g, k in G4:
                if m >= 2:
                    pe.wait_ge(s_b1e, m - 1)
                for b in range(k):
                    last = nc.tensor.transpose(psP[:, m % 2, b * P:(b + 1) * P], resT[:, (g + b) * P:(g + b + 1) * P], ident[:])
                last.then_inc(s_b1, 1)
            pe.wait_ge(s_x1, 1)
            for m, g, k in G4:
                if m >= 2:
                    pe.wait_ge(s_b2e, m - 1)
                for b in range(k):
                    last = nc.tensor.transpose(psP[:, m % 2, b * P:(b + 1) * P], x1[:, g + b, :], ident[:])
                last.then_inc(s_b2, 1)
            pe.wait_ge(s_b2e, len(G4))

            with pe.Fori(0, LAYERS) as l:
                pe.wait_ge(s_layer, l + 1)
                pe.wait_ge(s_lw, (l + 1) * 16 * (4 * HEADS + 1))
                nc.tensor.transpose(psP[:, 0, 0:P], w_gat[:], ident[:]).then_inc(s_lp, 1)
                pe.wait_ge(s_lpe, l * LPREP + 1)
                nc.tensor.matmul(psP[:, 1, 0:2 * HEADS], w_gatT[:], att_blk[:], start=True, stop=True).then_inc(s_lp, 1)
                pe.wait_ge(s_lpe, l * LPREP + 2)
                for m, g, k in G3:
                    if m >= 2:
                        pe.wait_ge(s_lpe, l * LPREP + 2 + 2 * (m - 1))
                    for b in range(k):
                        last = nc.tensor.matmul(psP[:, m % 2, b * HC:(b + 1) * HC], featT[:, (g + b) * P:(g + b + 1) * P],
                                                w_cat[:], start=True, stop=True)
                    last.then_inc(s_lp, 1)
                pe.wait_ge(s_wad, l + 1)
                pe.wait_ge(s_route, l + 1)
                stand(pe)
                general = pe.value_load(route[0:1, 0:1], min_val=0, max_val=1)
                g = pe.value_load(route[0:1, 1:2], min_val=0, max_val=LAYERS)
                f = pe.value_load(route[0:1, 2:3], min_val=0, max_val=LAYERS)
                with pe.If(general == 1):
                    with pe.Fori(0, NCH) as c:
                        t = g * NCH + c
                        pe.wait_ge(s_num, NCH + t + 1)
                        for h in range(HEADS):
                            last = nc.tensor.matmul(psS[:, h, 0:CH], wad[:, h, :], featT[:, bass.ds(c * CH, CH)],
                                                    start=True, stop=True)
                        last.then_inc(s_ad, 1)
                        clear_sums()
                        with pe.Fori(0, NB // RING) as i:
                            for j in range(RING):
                                pe.wait_ge(s_gw, t * NB + i * RING + j + 1)
                                for h in range(HEADS):
                                    last = nc.tensor.matmul(psO[HS * h:HS * h + HS, 0:CH], h_in[:, j, HS * h:HS * h + HS],
                                                            g_wts[:, j, h * CH:(h + 1) * CH],
                                                            start=False, stop=False, skip_group_check=True)
                                last.then_inc(s_gpv, 1)
                        pe.wait_ge(s_num, NCH + t + 2)
                        nc.tensor.matmul(psD[:, 0:CH], den_sel[:], g_num[:], start=True, stop=True).then_inc(s_den, 1)
                with pe.Else():
                    with pe.Fori(0, NR // AW) as i:
                        for h in range(HEADS):
                            pe.wait_ge(s_adre, (f * (NR // AW) + i) * HEADS + h + 1)
                            nc.tensor.matmul(psS[:, h, 0:AW], wad[:, h, :], featT[:, bass.ds(i * AW, AW)],
                                             start=True, stop=True).then_inc(s_adr, 1)
                    pe.wait_ge(s_adre, (f + 1) * (NR // AW) * HEADS + HEADS)
                    pe.wait_ge(s_part, (f + 1) * 4)
                    pe.wait_ge(s_low, (f + 1) * 2)
                    stand(pe)
                    W = DH + 1
                    with pe.Fori(0, NFC) as c:
                        t = f * NFC + c
                        pe.wait_ge(s_fsum, t * FB + 1)
                        for d in range(FB):
                            nc.tensor.matmul(acc[:, d, 0:500], zero16[:, 0:P], zero16[:, 0:500], start=True, stop=False,
                                             skip_group_check=True)
                        with pe.Fori(0, NB // RING) as i:
                            for j in range(RING):
                                n = t * NB + i * RING + j
                                blk = i * RING + j
                                pe.wait_ge(s_fc[j], 16 * (t * (NB // RING) + i + 1))
                                quad = parts[:, bass.ds(blk * HEADS, HEADS), :, W:2 * W]
                                for d in range(FB):
                                    for k in range(3):
                                        nc.tensor.matmul(acc[:, d, HEADS * 4 * W:HEADS * 5 * W], c16[:, j, d * P:(d + 1) * P],
                                                         quad[:, :, k, :], start=False, stop=False, skip_group_check=True)
                                for h in range(HEADS):
                                    pe.wait_ge(s_chosen, HEADS * n + h + 1)
                                    mine = parts[:, bass.ds(blk * HEADS + h, 1), :, :].rearrange("p a k f -> p (a k f)")
                                    for d in range(FB):
                                        w = chosen[:, (j * HEADS + h) % 10, d * P:(d + 1) * P]
                                        nc.tensor.matmul(acc[:, d, h * 4 * W:(h + 1) * 4 * W], w, mine[:, 0:4 * W],
                                                         start=False, stop=False, skip_group_check=True)
                                        last = nc.tensor.matmul(acc[:, d, h * 4 * W:h * 4 * W + 2 * W], w, mine[:, 4 * W:6 * W],
                                                                start=False, stop=False, skip_group_check=True)
                                    last.then_inc(s_head, 1)
                    pe.wait_ge(s_xn, f + 1)
                    for m, gg, k in G4:
                        if m >= 2:
                            pe.wait_ge(s_xte, f * len(G4) + m - 1)
                        for b in range(k):
                            last = nc.tensor.transpose(psP[:, m % 2, b * P:(b + 1) * P], x_next[:, gg + b, :], ident[:])
                        last.then_inc(s_xt, 1)
            pe.wait_ge(s_layer, LAYERS + 1)
            for m, g, k in G4:
                if m >= 2:
                    pe.wait_ge(s_fe, m - 1)
                for b in range(k):
                    last = nc.tensor.transpose(psP[:, m % 2, b * P:(b + 1) * P], featT[:, (g + b) * P:(g + b + 1) * P], ident[:])
                last.then_inc(s_f, 1)

        @block.scalar
        def _(act):
            act.sem_inc(s_exp, 2)
            act.sem_inc(s_trev, 1)
            act.sem_inc(s_adre, HEADS)
            act.sem_inc(s_fsum, 1)
            for j in range(RING):
                act.sem_inc(s_store[j], 32)
            act.wait_ge(s_init, 1)
            m = 0
            for _, g, k in G4:
                act.wait_ge(s_pm, m + 1)
                nc.scalar.copy(featT[0:D, g * P:(g + k) * P], psP[0:D, m % 2, 0:k * P]).then_inc(s_pe, 1)
                m += 1
            for o in (qT, kT):
                for c in range(NCH):
                    act.wait_ge(s_pm, m + 1)
                    nc.scalar.copy(o[:, c * CH:(c + 1) * CH], psP[:, m % 2, 0:CH]).then_inc(s_pe, 1)
                    m += 1
            for _, g, k in G4:
                act.wait_ge(s_pm, m + 1)
                nc.scalar.copy(v_sb[:, g:g + k, :].rearrange("p b (h c) -> p (b h) c", h=HEADS)[:, :, 0:DH],
                               psP[:, m % 2, 0:k * P].rearrange("p (a c) -> p a c", c=HS)[:, :, 0:DH]).then_inc(s_pe, 1)
                m += 1

            rows = counts[0:NC, :].rearrange("(c g p) d -> c p g d", g=4, p=TG)
            rows16 = counts16[0:NC, :].rearrange("(c g p) d -> c p g d", g=4, p=TG)
            with act.Fori(0, NCH) as c:
                act.wait_ge(s_qk, 2 * NB * c + 1)
                nc.scalar.copy(q_c[:], qT[:, bass.ds(c * CH, CH)]).then_inc(s_qc, 1)
                with act.Fori(0, NB // RING) as i:
                    for j in range(RING):
                        n = c * NB + i * RING + j
                        act.wait_ge(s_pv, n + 1)
                        for u in range(2):
                            act.wait_ge(s_qk, 2 * n + u + 2)
                            nc.scalar.activation(wts[:, j, u, :].rearrange("p (v f) -> p v f", v=2),
                                                 psS[:, 2 * u:2 * u + 2, 0:CH], ACT.Exp).then_inc(s_exp, 1)
                        act.wait_ge(s_tr, n + 1)
                        act.wait_ge(s_store[j], 32 * (c * (NB // RING) + i + 1))
                        nc.scalar.copy(cntT[0:TG, j, :], psP[0:TG, 0, :]).then_inc(s_trev, 1)
                        nc.scalar.copy(cntT16[0:TG, j, :], psP[0:TG, 0, :]).then_inc(s_trev, 1)
                        act.wait_ge(s_trev, 2 * n + 3)
                        act.dma_start(rows[bass.ds(c, 1), :, :, bass.ds((i * RING + j) * P, P)].rearrange("c p g d -> p (c g) d"),
                                      cntT[0:TG, j, :].rearrange("p (g d) -> p g d", g=4)).then_inc(s_store[j], 16)
                        act.dma_start(rows16[bass.ds(c, 1), :, :, bass.ds((i * RING + j) * P, P)].rearrange("c p g d -> p (c g) d"),
                                      cntT16[0:TG, j, :].rearrange("p (g d) -> p g d", g=4)).then_inc(s_store[j], 16)
            act.wait_ge(s_var, 1)
            nc.scalar.activation(stat[:, 2, :], stat[:, 1, :], ACT.Sqrt, bias=eps[:], scale=1.0 / D).then_inc(s_std, 1)
            for m, g, k in G4:
                act.wait_ge(s_b2, m + 1)
                nc.scalar.copy(featT[:, g * P:(g + k) * P], psP[:, m % 2, 0:k * P]).then_inc(s_b2e, 1)

            with act.Fori(0, LAYERS) as l:
                act.wait_ge(s_lp, l * (2 + len(G3)) + 1)
                nc.scalar.copy(w_gatT[:], psP[:, 0, 0:P]).then_inc(s_lpe, 1)
                act.wait_ge(s_lw, (l + 1) * 16 * (4 * HEADS + 1))
                nc.scalar.copy(w_cat[:, 0:P], w_gat[:])
                act.wait_ge(s_lp, l * (2 + len(G3)) + 2)
                nc.scalar.copy(w_cat[:, P:HC], psP[:, 1, 0:2 * HEADS]).then_inc(s_lpe, 1)
                for m, g, k in G3:
                    act.wait_ge(s_lp, l * (2 + len(G3)) + 3 + m)
                    ps = psP[:, m % 2, 0:k * HC].rearrange("p (b f) -> p b f", b=k)
                    nc.scalar.copy(h_sb[:, g:g + k, :].rearrange("p b (h c) -> p b h c", h=HEADS)[:, :, :, 0:DH],
                                   ps[:, :, 0:P].rearrange("p b (h c) -> p b h c", h=HEADS)[:, :, :, 0:DH]).then_inc(s_lpe, 1)
                    nc.scalar.copy(logit[:, g:g + k, :], ps[:, :, P:HC]).then_inc(s_lpe, 1)
                act.wait_ge(s_route, l + 1)
                stand(act)
                general = act.value_load(route[0:1, 0:1], min_val=0, max_val=1)
                g = act.value_load(route[0:1, 1:2], min_val=0, max_val=LAYERS)
                f = act.value_load(route[0:1, 2:3], min_val=0, max_val=LAYERS)
                with act.If(general == 1):
                    with act.Fori(0, NCH) as c:
                        t = g * NCH + c
                        act.wait_ge(s_ad, t + 1)
                        act.wait_ge(s_m, 4 * t + 1)
                        with act.Fori(0, NB // RING) as i:
                            for j in range(RING):
                                n = t * NB + i * RING + j
                                act.wait_ge(s_c[j], 48 * (2 * t * (NB // RING) + NB // RING + i + 1))
                                act.wait_ge(s_gpv, n + 1)
                                for h in range(HEADS):
                                    last = nc.scalar.activation(g_wts[:, j, h * CH:(h + 1) * CH], psS[:, h, 0:CH],
                                                                ACT.Identity, bias=as_in[:, j, h:h + 1])
                                last.then_inc(s_z, 1)
                                act.wait_ge(s_zm, 2 * n + 2)
                                nc.scalar.activation(g_wts[:, j, :], g_wts[:, j, :], ACT.Exp).then_inc(s_ez, 1)
                with act.Else():
                    act.wait_ge(s_sc, 2 * f + 1)
                    for k, scale in enumerate((1.0, 0.2)):
                        last = nc.scalar.activation(scale_s[:, :, :, k], neg_as[:], ACT.Exp, scale=-scale)
                    last.then_inc(s_sce, 1)
                    act.wait_ge(s_sc, 2 * f + 2)
                    nc.scalar.activation(scale_d[:], scale_d[:], ACT.Exp).then_inc(s_sce, 1)
                    for k in range(2):
                        for half in range(2):
                            act.wait_ge(s_term, 4 * f + 2 * k + half + 1)
                            a = slice(half * NB * HEADS // 2, (half + 1) * NB * HEADS // 2)
                            nc.scalar.copy(parts[:, a, k, :], terms[:, a, :]).then_inc(s_part, 1)
                    with act.Fori(0, NR // AW) as i:
                        for h in range(HEADS):
                            act.wait_ge(s_adr, (f * (NR // AW) + i) * HEADS + h + 1)
                            nc.scalar.copy(ad_row[:, h, bass.ds(i * AW, AW)], psS[:, h, 0:AW]).then_inc(s_adre, 1)
                    with act.Fori(0, NFC) as c:
                        t = f * NFC + c
                        act.wait_ge(s_head, HEADS * (t + 1) * NB + HEADS * RING)
                        act.wait_ge(s_comb, 4 * t + 1)
                        for d in range(FB):
                            nc.scalar.copy(sums[:, d, :], acc[:, d, 0:500]).then_inc(s_fsum, 1)
                    for m, gg, k in G4:
                        act.wait_ge(s_xt, f * len(G4) + m + 1)
                        nc.scalar.copy(featT[:, gg * P:(gg + k) * P], psP[:, m % 2, 0:k * P]).then_inc(s_xte, 1)
            act.wait_ge(s_var, 2)
            nc.scalar.activation(stat[:, 2, :], stat[:, 1, :], ACT.Sqrt, bias=eps[:], scale=1.0 / D).then_inc(s_std, 1)

        @block.vector
        def _(dve):
            steps = [0]

            def link(ins):
                steps[0] += 1
                ins.then_inc(s_chain, 1)
                dve.wait_ge(s_chain, steps[0])

            dve.sem_inc(s_cnt, RING)
            for s in (s_num, s_layer, s_cell):
                dve.sem_inc(s, 1)
            nc.vector.memset(x_sb[:], 0.0)
            nc.vector.memset(w_pad[:], 0.0)
            nc.vector.memset(w_gat[:], 0.0)
            nc.vector.memset(att_blk[:], 0.0)
            nc.vector.memset(bias[:], 0.0)
            nc.vector.memset(eps[:], 1e-5)
            nc.vector.memset(kT[:, NC:NR], 0.0)
            nc.vector.memset(featT[:, NC:NR], 0.0)
            nc.vector.memset(zeros[:], 0)
            nc.vector.memset(zero16[:], 0.0)
            nc.vector.memset(step_max[:], 0.0)
            nc.vector.memset(route_f[:], 0.0)
            link(nc.vector.memset(v_sb[:], 0.0))
            nc.vector.memset(v_sb[:].rearrange("p b (h c) -> p (b h) c", h=HEADS)[:, :, DH:DH + 1], 1.0).then_inc(s_init, 1)
            dve.wait_ge(s_edges, 32)
            dve.wait_ge(s_pool0, 6)
            link(nc.vector.tensor_copy(dump[:], dump_i[:]))
            link(nc.vector.scalar_tensor_tensor(key[:], dst_sb[:], float(NC), src_sb[:], ALU.mult, ALU.add))
            link(nc.vector.tensor_scalar(keyd[:], key[:], dump[:, 0:1], None, ALU.subtract))

            NDUP = 5
            with dve.Fori(0, GROUPS // 4) as i:
                for u in range(4):
                    g = i * 4 + u

                    def after(k):
                        dve.wait_ge(s_dup, g * NDUP + k)
                    kq = bass.ds(g * PLANES, PLANES)
                    dve.wait_ge(s_landed, g + 1)
                    nc.vector.tensor_tensor(diag[:, u % 2, :].rearrange("p (q e) -> p q e", q=PLANES),
                                            ident[0:EP, 0:EP].unsqueeze(1).to_broadcast([EP, PLANES, EP]),
                                            key[:, kq].unsqueeze(2).to_broadcast([EP, PLANES, EP]), ALU.mult).then_inc(s_diag, 1)
                    dve.wait_ge(s_keyrow, g + 1)
                    nc.vector.tensor_tensor(same[:].rearrange("p (q e) -> p q e", q=PLANES),
                                            psD[0:EP, 0:PLANES * EP].rearrange("p (q e) -> p q e", q=PLANES),
                                            key[:, kq].unsqueeze(2).to_broadcast([EP, PLANES, EP]), ALU.is_equal).then_inc(s_dup, 1)
                    after(1)
                    nc.vector.tensor_tensor(earlier[:].rearrange("p (q e) -> p q e", q=PLANES),
                                            same[:].rearrange("p (q e) -> p q e", q=PLANES),
                                            lower[:].unsqueeze(1).to_broadcast([EP, PLANES, EP]), ALU.mult).then_inc(s_dup, 1)
                    after(2)
                    nc.vector.tensor_reduce(n_earlier[:], earlier[:].rearrange("p (q e) -> p q e", q=PLANES), AX_X, ALU.add
                                            ).then_inc(s_dup, 1)
                    after(3)
                    nc.vector.scalar_tensor_tensor(kfirst[:], n_earlier[:], 0.0, keyd[:, kq], ALU.is_equal, ALU.mult).then_inc(s_dup, 1)
                    with nc.allow_low_precision("whole numbers up to 125"):
                        nc.vector.tensor_reduce(addend[:, u, :], same[:].rearrange("p (q e) -> p q e", q=PLANES), AX_X,
                                                ALU.add).then_inc(s_dup, 1)
                    after(5)
                    nc.vector.tensor_scalar(cell[:, u, :], kfirst[:], dump[:, 0:1], None, ALU.add).then_inc(s_cell, 1)

            dve.wait_ge(s_pe, len(G4))
            link(nc.vector.tensor_tensor(x_sb[:], x_sb[:], x_sb[:], ALU.add))

            def epilogue(c_now, floor, pv_done, num, den):
                dve.wait_ge(*pv_done)
                nc.vector.tensor_copy(num[:], psO[:, 0:CH]).then_inc(s_num, 1)
                dve.wait_ge(s_den, c_now + 1)
                nc.vector.tensor_scalar(den[:], psD[:, 0:CH], floor, None, ALU.add).then_inc(s_ep, 1)
                dve.wait_ge(s_ep, c_now * 3 + 1)
                nc.vector.reciprocal(den[:], den[:]).then_inc(s_ep, 1)
                dve.wait_ge(s_ep, c_now * 3 + 2)

            with dve.Fori(0, NCH) as c:
                with dve.Fori(0, NB // RING) as i:
                    for j in range(RING):
                        n = c * NB + i * RING + j
                        dve.wait_ge(s_plane[j], 16 * PLANES * (c * (NB // RING) + i + 1))
                        for q in (0, 2):
                            nc.vector.tensor_tensor(pl_in[:, j, q, :], pl_in[:, j, q, :], pl_in[:, j, q + 1, :], ALU.add
                                                    ).then_inc(s_pair, 1)
                        dve.wait_ge(s_pair, 2 * (n + 1))
                        dve.wait_ge(s_pv, n + 1)
                        stand(dve)
                        nc.vector.tensor_tensor_reduce(cnt[:, j, :], pl_in[:, j, 0, :], pl_in[:, j, 2, :], 1.0,
                                                       step_max[:, j:j + 1], ALU.add, ALU.max, step_max[:, j:j + 1]).then_inc(s_cnt, 1)
                        dve.wait_ge(s_cnt, n + 1 + RING)
                        for u in range(2):
                            dve.wait_ge(s_clip, 2 * n + u + 1)
                            w = wts[:, j, u, :].rearrange("p (v f) -> p v f", v=2)
                            nc.vector.tensor_tensor(w, w, cnt[:, j, :].unsqueeze(1).to_broadcast([P, 2, CH]), ALU.mult
                                                    ).then_inc(s_w, 1)
                epilogue(c, 1e-8, (s_pv, c * NB + NB + RING), num, den)
                nc.vector.tensor_tensor(resT[:, bass.ds(c * CH, CH)], num[:], den[:], ALU.mult).then_inc(s_ep, 1)
                dve.wait_ge(s_ep, c * 3 + 3)
                dve.sem_inc(s_res, 1)

            def layernorm(n, x_sb):
                link(nc.vector.tensor_reduce(stat[:, 0, :], x_sb, AX_X, ALU.add))
                link(nc.vector.tensor_scalar(stat[:, 0, :], stat[:, 0, :], 1.0 / D, None, ALU.mult))
                link(nc.vector.tensor_tensor(x_sb, x_sb, stat[:, 0, :].unsqueeze(2).to_broadcast([P, NB, D]), ALU.subtract))
                link(nc.vector.tensor_tensor(square, x_sb, x_sb, ALU.mult))
                nc.vector.tensor_reduce(stat[:, 1, :], square, AX_X, ALU.add).then_inc(s_var, 1)
                dve.wait_ge(s_std, n)
                link(nc.vector.reciprocal(stat[:, 3, :], stat[:, 2, :]))

            def wide(ap):
                return ap.rearrange("p b (h c) -> p b h c", h=HEADS)[:, :, :, 0:DH]

            def narrow(ap):
                return ap.rearrange("p b (h c) -> p b h c", h=HEADS)

            for m, g, k in G4:
                dve.wait_ge(s_b1, m + 1)
                nc.vector.tensor_tensor(narrow(x_sb[:, g:g + k, :]), wide(psP[:, m % 2, 0:k * P].rearrange("p (b f) -> p b f", b=k)),
                                        narrow(x_sb[:, g:g + k, :]), ALU.add).then_inc(s_b1e, 1)
            dve.wait_ge(s_b1e, len(G4))
            link(nc.vector.memset(x1, 0.0))
            layernorm(1, x_sb[:])
            nc.vector.tensor_tensor(wide(x1), narrow(x_sb[:]),
                                    stat[:, 3, :].unsqueeze(2).unsqueeze(3).to_broadcast([P, NB, HEADS, DH]), ALU.mult).then_inc(s_x1, 1)

            link(nc.vector.tensor_reduce(extreme[:, 2 * HEADS:2 * HEADS + 1], step_max[:], AX_X, ALU.max))

            def heads_of(flat):
                return flat.rearrange("p (h f) -> p h f", h=HEADS)

            with dve.Fori(0, LAYERS) as l:
                dve.wait_ge(s_lpe, l * LPREP + 2)
                for h in range(HEADS):
                    last = nc.vector.tensor_scalar(wad[:, h, :], ones[:], w_cat[:, P + HEADS + h:P + HEADS + h + 1], None, ALU.mult)
                last.then_inc(s_wad, 1)
                dve.wait_ge(s_lpe, (l + 1) * LPREP)
                nc.vector.tensor_scalar(neg_as[:], logit[:, :, 0:HEADS], -1.0, None, ALU.mult).then_inc(s_lay, 1)
                nc.vector.tensor_reduce(extreme[:, 0:HEADS], logit[:, :, 0:HEADS].rearrange("p b h -> p h b"), AX_X, ALU.max
                                        ).then_inc(s_lay, 1)
                dve.wait_ge(s_lay, 6 * l + 2)
                nc.vector.tensor_reduce(extreme[:, HEADS:2 * HEADS], neg_as[:].rearrange("p b h -> p h b"), AX_X, ALU.max
                                        ).then_inc(s_ext, 1)
                dve.wait_ge(s_ar, l + 1)
                nc.vector.tensor_tensor(spread[:, 0:HEADS], extremes[:, 0:HEADS], extremes[:, HEADS:2 * HEADS], ALU.add).then_inc(s_lay, 1)
                nc.vector.tensor_scalar(spread[:, HEADS:HEADS + 1], extremes[:, 2 * HEADS:2 * HEADS + 1], SPREAD / COUNT, None,
                                        ALU.mult).then_inc(s_lay, 1)
                dve.wait_ge(s_lay, 6 * l + 4)
                nc.vector.tensor_reduce(spread[:, HEADS + 1:HEADS + 2], spread[:, 0:HEADS + 1], AX_X, ALU.max).then_inc(s_lay, 1)
                dve.wait_ge(s_lay, 6 * l + 5)
                nc.vector.tensor_scalar(route_f[:, 0:1], spread[0:1, HEADS + 1:HEADS + 2], SPREAD, None, ALU.is_gt).then_inc(s_lay, 1)
                dve.wait_ge(s_lay, 6 * l + 6)
                nc.vector.tensor_copy(route[:], route_f[:]).then_inc(s_route, 1)
                dve.wait_ge(s_route, l + 1)
                stand(dve)
                general = dve.value_load(route[0:1, 0:1], min_val=0, max_val=1)
                g = dve.value_load(route[0:1, 1:2], min_val=0, max_val=LAYERS)
                f = dve.value_load(route[0:1, 2:3], min_val=0, max_val=LAYERS)
                nc.vector.tensor_tensor(route_f[:, 1:2], route_f[:, 1:2], route_f[:, 0:1], ALU.add).then_inc(s_lay2, 1)
                nc.vector.scalar_tensor_tensor(route_f[:, 2:3], route_f[:, 2:3], 1.0, route_f[:, 0:1], ALU.add, ALU.subtract
                                               ).then_inc(s_lay2, 1)
                dve.wait_ge(s_lay2, 2 * l + 2)
                stand(dve)
                with dve.If(general == 1):
                    with dve.Fori(0, NCH) as c:
                        t = g * NCH + c
                        dve.wait_ge(s_amax, t + 1)
                        nc.vector.memset(run_max, -2.0 * BIG).then_inc(s_rm, 1)
                        with dve.Fori(0, NB // RING) as i:
                            for j in range(RING):
                                base = t * MAXOPS + 1 + (1 + HEADS) * (i * RING + j)
                                dve.wait_ge(s_c[j], 48 * (2 * t * (NB // RING) + i + 1))
                                dve.wait_ge(s_rm, base)
                                nc.vector.tensor_scalar(absent[:], c_in[:, j, :], 0.0, -BIG, ALU.is_equal, ALU.mult).then_inc(s_rm, 1)
                                dve.wait_ge(s_rm, base + 1)
                                for h in range(HEADS):
                                    r = run_max[:, h * CH:(h + 1) * CH]
                                    nc.vector.scalar_tensor_tensor(r, absent[:], as_in[:, j, h:h + 1], r, ALU.add, ALU.max
                                                                   ).then_inc(s_rm, 1)
                        dve.wait_ge(s_amax, t + 2)
                        dve.wait_ge(s_ad, t + 1)
                        nc.vector.tensor_tensor(heads_of(m_row), psS[:, :, 0:CH], heads_of(all_max), ALU.add).then_inc(s_m, 1)
                        dve.wait_ge(s_m, 4 * t + 1)
                        nc.vector.scalar_tensor_tensor(m_row, m_row, 0.2, m_row, ALU.mult, ALU.max).then_inc(s_m, 1)
                        nc.vector.tensor_scalar(all_max, all_max, -0.5 * BIG, None, ALU.is_gt).then_inc(s_m, 1)
                        dve.wait_ge(s_m, 4 * t + 3)
                        nc.vector.tensor_tensor(m_row, m_row, all_max, ALU.mult).then_inc(s_m, 1)
                        dve.wait_ge(s_m, 4 * t + 4)
                        stand(dve)
                        with dve.Fori(0, NB // RING) as i:
                            for j in range(RING):
                                n = t * NB + i * RING + j
                                w = g_wts[:, j, :]
                                dve.wait_ge(s_z, n + 1)
                                nc.vector.scalar_tensor_tensor(w, w, 0.2, w, ALU.mult, ALU.max).then_inc(s_zm, 1)
                                dve.wait_ge(s_zm, 2 * n + 1)
                                nc.vector.tensor_tensor(w, w, m_row, ALU.subtract).then_inc(s_zm, 1)
                                dve.wait_ge(s_ez, n + 1)
                                dve.wait_ge(s_c[j], 48 * (2 * t * (NB // RING) + NB // RING + i + 1))
                                nc.vector.scalar_tensor_tensor(heads_of(w), heads_of(w), 1.0,
                                                               c_in[:, j, :].unsqueeze(1).to_broadcast([P, HEADS, CH]),
                                                               ALU.min, ALU.mult).then_inc(s_gw, 1)
                        epilogue(NCH + t, 1e-16, (s_gpv, t * NB + NB + RING), g_num, g_den)
                        o = outT[:, bass.ds(c * CH, CH)]
                        nc.vector.tensor_tensor(g_num[:], g_num[:], g_den[:], ALU.mult).then_inc(s_ep, 1)
                        dve.wait_ge(s_ep, (NCH + t) * 3 + 3)
                        nc.vector.tensor_scalar(o, g_num[:], bias[:, 0:1], 0.0, ALU.add, ALU.max).then_inc(s_relu, 1)
                    dve.wait_ge(s_relu, (g + 1) * NCH)
                    nc.vector.tensor_copy(featT[:, 0:NC], outT[:, 0:NC]).then_inc(s_layer, 1)

                with dve.Else():
                    W = DH + 1
                    top = extremes[:, 0:HEADS].unsqueeze(1).to_broadcast([P, NB, HEADS])
                    own = [0]

                    def link2(ins, k):
                        own[0] += 1
                        ins.then_inc(s_own, 1)
                        dve.wait_ge(s_own, OWN * f + own[0])
                    nc.vector.tensor_tensor(neg_as[:], neg_as[:], top, ALU.add).then_inc(s_sc, 1)
                    link2(nc.vector.tensor_tensor(scale_d[:, 0], logit[:, :, HEADS:2 * HEADS], top, ALU.add), 0)
                    link2(nc.vector.tensor_scalar(scale_d[:, 1], scale_d[:, 0], -0.8, 0.0, ALU.mult, ALU.min), 0)
                    nc.vector.tensor_scalar(scale_d[:, 0], scale_d[:, 0], 0.8, 0.0, ALU.mult, ALU.min).then_inc(s_sc, 1)
                    dve.wait_ge(s_sce, 2 * f + 1)
                    halves = [slice(half * NB * HEADS // 2, (half + 1) * NB * HEADS // 2) for half in range(2)]
                    hv = h_sb[:].rearrange("p b (h c) -> p (b h) c", h=HEADS)[:, :, 0:W]
                    for half, a in enumerate(halves):
                        n_a = a.stop - a.start
                        nc.vector.tensor_tensor(terms[:, a, :].rearrange("p a (k f) -> p a k f", k=2),
                                                hv[:, a, :].unsqueeze(2).to_broadcast([P, n_a, 2, W]),
                                                scale_s[:].rearrange("p b h k -> p (b h) k")[:, a, :].unsqueeze(3)
                                                .to_broadcast([P, n_a, 2, W]), ALU.mult).then_inc(s_term, 1)
                    for k in range(2):
                        for half, a in enumerate(halves):
                            dve.wait_ge(s_part, 4 * f + 2 * k + half + 1)
                            o = terms[:, a, :] if k == 0 else parts[:, a, 2, :]
                            ins = nc.vector.tensor_tensor(o, terms[:, a, :], parts[:, a, k, :], ALU.subtract)
                            ins.then_inc(s_term if k == 0 else s_low, 1)
                    dve.wait_ge(s_sce, 2 * f + 2)
                    link2(nc.vector.tensor_scalar(neg_as[:], logit[:, :, 0:HEADS], -1.0, None, ALU.mult), 0)
                    dve.wait_ge(s_adre, (f + 1) * (NR // AW) * HEADS + HEADS)
                    stand(dve)
                    with dve.Fori(0, NFC) as c:
                        with dve.Fori(0, NB // RING) as i:
                            for j in range(RING):
                                t = f * NFC + c
                                n = t * NB + i * RING + j
                                dve.wait_ge(s_fc[j], 16 * (t * (NB // RING) + i + 1))
                                for h in range(HEADS):
                                    dve.wait_ge(s_head, HEADS * n + h + 1 + HEADS * RING - 10)
                                    nc.vector.scalar_tensor_tensor(chosen[:, (j * HEADS + h) % 10, :],
                                                                   ad_row[:, h, bass.ds(c * FC, FC)],
                                                                   one(neg_as[:, bass.ds(i * RING + j, 1), h:h + 1]),
                                                                   c16[:, j, :], ALU.is_ge, ALU.mult).then_inc(s_chosen, 1)
                    dve.wait_ge(s_comb, 4 * (f + 1) * NFC + 1)
                    link2(nc.vector.tensor_scalar(rden[:], total[:, :, :, DH:W].rearrange("p b h o -> p b (h o)"), 1e-30, None, ALU.max), 0)
                    link2(nc.vector.reciprocal(rden[:], rden[:]), 0)
                    link2(nc.vector.tensor_tensor(total[:, :, :, 0:DH], total[:, :, :, 0:DH],
                                                  rden[:].unsqueeze(3).to_broadcast([P, NB, HEADS, DH]), ALU.mult), 0)
                    link2(nc.vector.tensor_tensor(total[:, :, :, 0:DH], total[:, :, :, 0:DH],
                                                  heads(bias_row[:]).unsqueeze(1).to_broadcast([P, NB, HEADS, DH]), ALU.add), 0)
                    nc.vector.memset(x_next.rearrange("p b (h c) -> p (b h) c", h=HEADS)[:, :, DH:HS], 0.0)
                    nc.vector.tensor_scalar(wide(x_next), total[:, :, :, 0:DH], 0.0, None, ALU.max).then_inc(s_xn, 1)
                    assert own[0] == OWN
                    dve.wait_ge(s_xte, (f + 1) * len(G4))
                    dve.sem_inc(s_layer, 1)

            for m, g, k in G4:
                dve.wait_ge(s_f, m + 1)
                nc.vector.tensor_tensor(narrow(y_sb[:, g:g + k, :]), wide(psP[:, m % 2, 0:k * P].rearrange("p (b f) -> p b f", b=k)),
                                        wide(x1[:, g:g + k, :]), ALU.add).then_inc(s_fe, 1)
            dve.wait_ge(s_fe, len(G4))
            layernorm(2, y_sb)
            nc.vector.tensor_tensor(y_sb, y_sb, stat[:, 3, :].unsqueeze(2).to_broadcast([P, NB, D]), ALU.mult).then_inc(s_fin, 1)


_INS = ["x", "src", "dst", "L0_gnn_qW", "L0_gnn_kW", "L0_gnn_vW", "L1_gnn_W", "L1_gnn_att_src", "L1_gnn_att_dst", "L1_gnn_bias"]


def kernel(**inputs):
    import numpy as _np
    import concourse.bacc as _bacc
    from concourse import mybir as _mybir
    from concourse.bass_utils import run_bass_kernel_spmd as _run

    nc = _bacc.Bacc("TRN2", target_bir_lowering=False, num_devices=1)
    arrays, args = {}, []
    for name in _INS:
        a = _np.ascontiguousarray(inputs[name])
        arrays[f"in_{name}_dram"] = a
        args.append(nc.dram_tensor(f"in_{name}_dram", a.shape, _mybir.dt.from_np(a.dtype), kind="ExternalInput").ap())
    x = inputs["x"]
    args.append(nc.dram_tensor("out_0_dram", x.shape, _mybir.dt.float32, kind="ExternalOutput").ap())
    build(nc, *args)
    r = _run(nc, [arrays], core_ids=[0])
    return r.results[0]["out_0_dram"]
```

```python
from contextlib import ExitStack

import concourse.bass as bass
from concourse import mybir

F32 = mybir.dt.float32
BF16 = mybir.dt.bfloat16
I32 = mybir.dt.int32
U32 = mybir.dt.uint32
U16 = mybir.dt.uint16
ALU = mybir.AluOpType
ACT = mybir.ActivationFunctionType
AX_X = mybir.AxisListType.X
RMAX = bass.bass_isa.ReduceOp.max

P = 128
HEADS = 4
HS = 32
PLANES = 4
RING = 5
BIG = 1.0e30
LAYERS = 3
SPREAD = 60.0
COUNT = 256.0
CLIPPED = 3
SKEW = 6
E_HI = 22026.465794806718


def build(nc, x, src, dst, q_w, k_w, v_w, gat_w, att_src, att_dst, gat_b, out):
    N, D = x.shape
    E = src.shape[0]
    DH = D // HEADS
    NB = -(-N // P)
    NR = NB * P
    FB = 5
    FC = FB * P
    NFC = NB // FB
    CH = 448
    NCH = -(-N // CH)
    NC = NCH * CH
    TAIL = N - (NB - 1) * P
    EP = 125
    ET = E // EP
    SET = 4
    SETS = ET // SET
    EARLY = 16
    EARLY_SETS = EARLY * sum(range(PLANES)) // SET
    INTO = [SETS - EARLY_SETS + EARLY * (PLANES - 1 - q) for q in range(PLANES)]
    CELLS = NR * NR
    HC = HEADS * HS + 2 * HEADS
    STEPS = NB // FB * NB
    AW = 400
    NA = NR // AW
    UR = 10
    ZN = CELLS // P // NR
    assert EP * ET == E and SETS % 4 == 0 and EARLY_SETS % 4 == 0 and SET == PLANES and sum(INTO) == ET and NB % RING == 0 and CELLS + EP < 2 ** 24

    with ExitStack() as ctx:
        def sb(name, shape, dt, span=ctx):
            return span.enter_context(nc.sbuf_tensor(name, shape, dt))

        def stage():
            return ExitStack()

        def psum(name, shape):
            return ctx.enter_context(nc.psum_tensor(name, shape, F32))

        def sem(name):
            return ctx.enter_context(nc.semaphore(name))

        plane = [nc.dram_tensor(f"plane{i}", (CELLS + P, 1), U16).ap() for i in range(PLANES)]
        plane_v = [a[0:CELLS, :].rearrange("(b p f) o -> b p (f o)", p=P, f=NR) for a in plane]
        counts = nc.dram_tensor("counts", (NR, NR), F32).ap()
        parts_q = nc.dram_tensor("parts_q", (P, 2, HEADS, NR), BF16).ap()
        parts_k = nc.dram_tensor("parts_k", (P, 2, HEADS, NR), BF16).ap()
        ROWS_Q, ROWS_K = ((0, 0, 1, 1), (0, 2, 1, 2)), ((0, 1, 0, 1), (2, 0, 2, 1))
        counts16 = nc.dram_tensor("counts16", (NR, NR), BF16).ap()

        ident = sb("ident", [P, P], F32)
        ident16 = sb("ident16", [P, P], BF16)
        den_sel = sb("den_sel", [P, P], F32)
        ones = sb("ones", [P, P], F32)
        zero16 = sb("zero16", [P, 512], BF16)
        feat_x1 = sb("feat_x1", [P, 2 * NR], F32)
        featT = feat_x1[:, 0:NR]
        x1 = feat_x1[:, NR:].rearrange("p (b f) -> p b f", f=P)
        outT = sb("outT", [P, NR], F32)
        total = outT[:, 0:NB * HEADS * (DH + 1)].rearrange("p (b h f) -> p b h f", h=HEADS, f=DH + 1)
        v_sb = sb("v_sb", [P, NB, P], F32)
        h_sb = v_sb
        sums0 = v_sb
        square = outT[:, 0:NB * D].rearrange("p (b f) -> p b f", f=D)
        w_gat = sb("w_gat", [P, P], F32)
        w_gatT = sb("w_gatT", [P, P], F32)
        att_blk = sb("att_blk", [P, 2 * HEADS], F32)
        bias = sb("bias", [P, 1], F32)
        eps = sb("eps", [P, 1], F32)
        w_cat = sb("w_cat", [P, HC], F32)
        wad = sb("wad", [P, HEADS, P], F32)
        logit = sb("logit", [P, NB, 2 * HEADS], F32)
        stat = sb("stat", [P, 4, NB], F32)
        step_max = sb("step_max", [P, RING], F32)
        extreme = sb("extreme", [P, 2 * HEADS + 1], F32)
        extremes = sb("extremes", [P, 2 * HEADS + 1], F32)
        spread = sb("spread", [P, HEADS + 2], F32)
        rden = sb("rden", [P, NB, HEADS], F32)
        minus10 = sb("minus10", [P, 1], F32)
        plus10 = sb("plus10", [P, 1], F32)
        route_f = sb("route_f", [1, 3], F32)
        route = sb("route", [1, 3], I32)

        early = ctx.enter_context(stage())
        x_sb = sb("x_sb", [P, NB, D], F32, early)
        with stage() as span:
            piece = sb("piece", [P, 2, 3, NR], BF16, span)
            w_pad = sb("w_pad", [P, 3, P], F32, span)
            zeros = sb("zeros", [P, NR], U16, span)
            lower = sb("lower", [EP, EP], BF16, span)
            dump_i = sb("dump_i", [EP, 1], I32, span)
            dump = sb("dump", [EP, 1], F32, span)
            src_sb = sb("src_sb", [EP, ET], I32, span)
            dst_sb = sb("dst_sb", [EP, ET], I32, span)
            key = sb("key", [EP, ET], F32, span)
            keyd = sb("keyd", [EP, ET], F32, span)
            diag = sb("diag", [EP, 2, SET * EP], F32, span)
            same = sb("same", [EP, 2, SET * EP], BF16, span)
            earlier = sb("earlier", [EP, 2, SET * EP], BF16, span)
            n_earlier = sb("n_earlier", [EP, 2, SET], F32, span)
            kfirst = sb("kfirst", [EP, 2, SET], F32, span)
            cell = sb("cell", [EP, 4, SET], U32, span)
            addend = sb("addend", [EP, 4, SET], U16, span)
            rest = sb("rest", [P, 2, AW], F32, span)
        with stage() as span:
            q_first = sb("q_first", [P, HEADS, NR], BF16, span)[:]
            q_second = feat_x1[:].bitcast(BF16).rearrange("p (h n) -> p h n", h=HEADS)
            v_in = sb("v_in", [P, RING, P], F32, span)
            k_in = sb("k_in", [P, RING, 2, HEADS, P], BF16, span)
            pl_in = sb("pl_in", [P, RING, PLANES, FC], U16, span)
            cnt = sb("cnt", [P, RING, FC], F32, span)
            cnt16 = sb("cnt16", [P, RING, FC], BF16, span)
            cntT = sb("cntT", [P, FB, RING * P], BF16, span)
            wts = sb("wts", [P, UR, FC], F32, span)
        early.close()

        with stage() as span:
            g_hold = sb("g_hold", [P, NB * P], F32, span)
            h_in = sb("h_in", [P, RING, P], F32, span)
            c_in = sb("c_in", [P, RING, CH], F32, span)
            as_in = sb("as_in", [P, RING, HEADS], F32, span)
            g_wts = sb("g_wts", [P, RING, HEADS * CH], F32, span)
            g_num = sb("g_num", [P, CH], F32, span)
            g_den = sb("g_den", [P, CH], F32, span)
            absent = sb("absent", [P, CH], F32, span)
            r_pl = sb("r_pl", [P, PLANES, FC], U16, span)
            r_cnt = sb("r_cnt", [P, FC], F32, span)
            r_out = sb("r_out", [P, FC], F32, span)
            run_max = sb("run_max", [P, HEADS * CH], F32, span)[:]
            all_max = sb("all_max", [P, HEADS * CH], F32, span)[:]
            m_row = sb("m_row", [P, HEADS * CH], F32, span)[:]

        with stage() as span:
            room = sb("room", [P, NB * HEADS * 2 * (DH + 1)], F32, span)
            terms = room[:].rearrange("p (a f) -> p a f", f=2 * (DH + 1))
            sums = room[:, 0:FB * 500].rearrange("p (d f) -> p d f", d=FB)
            x_next = room[:, 0:NB * P].rearrange("p (b f) -> p b f", f=P)
            y_sb = room[:, 0:NB * D].rearrange("p (b f) -> p b f", f=D)
            parts = sb("parts", [P, NB * HEADS, 3, 2 * (DH + 1)], BF16, span)
            neg_as = sb("neg_as", [P, NB, HEADS], F32, span)
            scale_s = sb("scale_s", [P, NB, HEADS, 2], F32, span)
            scale_d = sb("scale_d", [P, 2, NB, HEADS], F32, span)
            ad_row = sb("ad_row", [P, HEADS, NR], F32, span)
            c16 = sb("c16", [P, RING, FC], BF16, span)
            chosen = sb("chosen", [P, UR, FC], BF16, span)

        acc = psum("acc", [P, 8, 512])
        psS = acc[:, 0:4]
        psO = acc[:, 4]
        psP = acc[:, 5:7]
        psK = [acc[:, 4], acc[:, 7]]
        psD = acc[:, 7]

        psU = [acc[:, 0:2, 0:FC // 2], acc[:, 2:4, 0:FC // 2]]
        psV = acc[:, 4:8:2, 0:FC // 2]
        psT = acc[:, 5].bitcast(BF16)

        G4 = [(m, g, min(4, NB - g)) for m, g in enumerate(range(0, NB, 4))]
        G3 = [(m, g, min(3, NB - g)) for m, g in enumerate(range(0, NB, 3))]
        LPREP = 2 + 2 * len(G3)
        CHAINED = 5
        MAXOPS = 1 + NB * (1 + HEADS)

        s_init = sem("s_init")
        s_pool0 = sem("s_pool0")
        s_edges = sem("s_edges")
        s_x = sem("s_x")
        s_zero = [[sem(f"s_zero{i}{u}") for u in "ab"] for i in range(PLANES)]
        s_chain = sem("s_chain")
        s_diag = sem("s_diag")
        s_key = sem("s_key")
        s_keyrow = sem("s_keyrow")
        s_dup = sem("s_dup")
        s_cell = sem("s_cell")
        s_same = sem("s_same")
        s_landed = sem("s_landed")
        s_scat = [sem(f"s_scat{i}") for i in range(PLANES)]
        s_pm = sem("s_pm")
        s_pe = sem("s_pe")
        s_plane = [sem(f"s_plane{i}") for i in range(RING)]
        s_kv = [sem(f"s_kv{i}") for i in range(RING)]
        s_pair = sem("s_pair")
        s_cnt = sem("s_cnt")
        s_qc = sem("s_qc")
        s_qk = sem("s_qk")
        s_exp = sem("s_exp")
        s_clip = sem("s_clip")
        s_w = sem("s_w")
        s_wlast = sem("s_wlast")
        s_pv = sem("s_pv")
        s_tr = sem("s_tr")
        s_trev = sem("s_trev")
        s_store = sem("s_store")
        s_rsum, s_rpl, s_rop, s_rtr, s_rev, s_rst = (sem(n) for n in ("s_rsum", "s_rpl", "s_rop", "s_rtr", "s_rev", "s_rst"))
        s_proj = sem("s_proj")
        s_first = sem("s_first")
        s_second = sem("s_second")
        s_rest = sem("s_rest")
        s_piece = sem("s_piece")
        s_parts = sem("s_parts")
        s_read = sem("s_read")
        s_c16 = sem("s_c16")
        s_tot = sem("s_tot")
        s_num = sem("s_num")
        s_den = sem("s_den")
        s_ep = sem("s_ep")
        s_b1 = sem("s_b1")
        s_b1e = sem("s_b1e")
        s_x1 = sem("s_x1")
        s_b2 = sem("s_b2")
        s_b2e = sem("s_b2e")
        s_lw = sem("s_lw")
        s_lp = sem("s_lp")
        s_lpe = sem("s_lpe")
        s_wad = sem("s_wad")
        s_ad = sem("s_ad")
        s_c = [sem(f"s_c{i}") for i in range(RING)]
        s_rm = sem("s_rm")
        s_amax = sem("s_amax")
        s_m = sem("s_m")
        s_z = sem("s_z")
        s_zm = sem("s_zm")
        s_ez = sem("s_ez")
        s_gw = sem("s_gw")
        s_gpv = sem("s_gpv")
        s_relu = sem("s_relu")
        s_layer = sem("s_layer")
        s_f = sem("s_f")
        s_fe = sem("s_fe")
        s_var = sem("s_var")
        s_std = sem("s_std")
        s_lay = sem("s_lay")
        s_lay2 = sem("s_lay2")
        s_own = sem("s_own")
        s_route = sem("s_route")
        s_ext = sem("s_ext")
        s_ar = sem("s_ar")
        s_sc = sem("s_sc")
        s_sce = sem("s_sce")
        s_term = sem("s_term")
        s_part = sem("s_part")
        s_low = sem("s_low")
        s_adr = sem("s_adr")
        s_adre = sem("s_adre")
        s_fc = [sem(f"s_fc{i}") for i in range(RING)]
        s_chosen = sem("s_chosen")
        s_sign = sem("s_sign")
        s_chlast = sem("s_chlast")
        s_head = sem("s_head")
        s_fsum = sem("s_fsum")
        s_comb = sem("s_comb")
        s_xn = sem("s_xn")
        s_xt = sem("s_xt")
        s_xte = sem("s_xte")
        s_stand = sem("s_stand")
        s_fin = sem("s_fin")
        s_out = sem("s_out")

        def heads(ap):
            return ap.rearrange("p (h c) -> p h c", h=HEADS)

        def stand(eng):
            eng.sem_inc(s_stand, 1)

        def one(ap):
            return ap.rearrange("p b f -> p (b f)")

        block = ctx.enter_context(nc.Block())

        @block.sync
        def _(sp):
            sp.dma_start(src_sb[:], src.rearrange("(p t) -> p t", p=EP)).then_inc(s_edges, 16)
            sp.dma_start(dst_sb[:], dst.rearrange("(p t) -> p t", p=EP)).then_inc(s_edges, 16)
            sp.wait_ge(s_init, 1)
            sp.dma_start(x_sb[:, 0:NB - 1, :], x[0:(NB - 1) * P, :].rearrange("(b p) d -> p b d", p=P)).then_inc(s_x, 16)
            sp.dma_start(x_sb[0:TAIL, NB - 1, :], x[(NB - 1) * P:N, :]).then_inc(s_x, 16)
            for j, w in enumerate((q_w, k_w, v_w)):
                sp.dma_start(heads(w_pad[0:D, j, :])[:, :, 0:DH], heads(w)).then_inc(s_x, 16)
            for i in range(PLANES):
                flat = plane[i][0:CELLS, :].rearrange("(p a f) o -> p a (f o)", p=P, a=ZN)
                for u in range(2):
                    sp.dma_start(flat[:, u, :], zeros[:]).then_inc(s_zero[i][u], 16)
                with sp.Fori(1, ZN // 2) as k:
                    for u in range(2):
                        sp.wait_ge(s_zero[i][u], 16 * k)
                        sp.dma_start(one(flat[:, bass.ds(2 * k + u, 1), :]), zeros[:]).then_inc(s_zero[i][u], 16)
                for a in range(ZN // 2 * 2, ZN):
                    sp.wait_ge(s_zero[i][a % 2], 16 * (a // 2))
                    sp.dma_start(flat[:, a, :], zeros[:]).then_inc(s_zero[i][a % 2], 16)

            for t, (rows_of, dest) in enumerate(((ROWS_Q, parts_q), (ROWS_K, parts_k))):
                sp.wait_ge(s_piece, (t + 1) * NA)
                for k in range(2):
                    for g in range(4):
                        for h in range(HEADS):
                            sp.dma_start(dest[g * HS:(g + 1) * HS, k, h, :], piece[h * HS:(h + 1) * HS, t, rows_of[k][g], :]
                                         ).then_inc(s_parts, 16)
            sp.wait_ge(s_parts, 16 * 64)

            sp.dma_start(q_first, parts_q[:, 0, :, :]).then_inc(s_qc, 16)
            sp.dma_start(q_second, parts_q[:, 1, :, :]).then_inc(s_qc, 16)
            with sp.Fori(0, NFC) as c:
                with sp.Fori(0, NB // RING) as i:
                    for j in range(RING):
                        n = c * NB + i * RING + j
                        blk = i * RING + j
                        sp.wait_ge(s_qk, HEADS * (n + 1))
                        sp.dma_start(k_in[:, j].rearrange("p k h f -> p (k h) f"),
                                     parts_k.rearrange("p k h n -> p (k h) n")[:, :, bass.ds(blk * P, P)]).then_inc(s_kv[j], 16)
                        sp.wait_ge(s_pv, HEADS * (n + 1))
                        sp.dma_start(v_in[:, j, :], one(v_sb[:, bass.ds(blk, 1), :])).then_inc(s_kv[j], 16)
                        sp.wait_ge(s_cnt, n + 1)
                        for q in range(PLANES):
                            sp.wait_ge(s_scat[q], 16 * INTO[q])
                            sp.dma_start(pl_in[:, j, q, :],
                                         plane_v[q][bass.ds(blk, 1), :, bass.ds(c * FC, FC)].rearrange("b p f -> p (b f)")
                                         ).then_inc(s_plane[j], 16)

            sp.wait_ge(s_store, 16 * (STEPS // RING) + 16)
            with sp.Fori(0, LAYERS) as l:
                sp.wait_ge(s_b2e, len(G4))
                sp.wait_ge(s_layer, l + 1)
                for h in range(HEADS):
                    rows = slice(HS * h, HS * h + DH)
                    sp.dma_start(heads(w_gat[rows, :])[:, :, 0:DH],
                                 gat_w[bass.ds(l, 1), DH * h:DH * h + DH, :].rearrange("l k (h c) -> k (l h) c", h=HEADS)
                                 ).then_inc(s_lw, 16)
                    sp.dma_start(att_blk[rows, h:h + 1],
                                 att_src[bass.ds(l, 1), h:h + 1, :].rearrange("l h c -> c (l h)")).then_inc(s_lw, 16)
                    sp.dma_start(att_blk[rows, HEADS + h:HEADS + h + 1],
                                 att_dst[bass.ds(l, 1), h:h + 1, :].rearrange("l h c -> c (l h)")).then_inc(s_lw, 16)
                    sp.dma_start(bias[rows, :],
                                 gat_b[bass.ds(l, 1), DH * h:DH * h + DH].rearrange("l c -> c l")).then_inc(s_lw, 16)

                sp.wait_ge(s_route, l + 1)
                stand(sp)
                general = sp.value_load(route[0:1, 0:1], min_val=0, max_val=1)
                g = sp.value_load(route[0:1, 1:2], min_val=0, max_val=LAYERS)
                f = sp.value_load(route[0:1, 2:3], min_val=0, max_val=LAYERS)
                with sp.If(general == 1):
                    sp.wait_ge(s_adre, (l + 1) * (NR // AW) * HEADS + HEADS)
                    stand(sp)
                    with sp.Fori(0, NFC) as c:
                        with sp.Fori(0, NB) as b:
                            sp.wait_ge(s_rsum, g * STEPS + c * NB + b + 1)
                            for q in range(PLANES):
                                sp.dma_start(r_pl[:, q, :],
                                             plane_v[q][bass.ds(b, 1), :, bass.ds(c * FC, FC)].rearrange("b p f -> p (b f)")
                                             ).then_inc(s_rpl, 16)
                    sp.wait_ge(s_rst, 16 * (g + 1) * STEPS + 16)
                    stand(sp)
                    counts_v = counts.rearrange("(b p) f -> b p f", p=P)

                    def load(c, blk, j):
                        sp.dma_start(c_in[:, j, :], counts_v[bass.ds(blk, 1), :, bass.ds(c * CH, CH)]
                                     .rearrange("b p f -> p (b f)")).then_inc(s_c[j], 16)
                        sp.dma_start(h_in[:, j, :], one(h_sb[:, bass.ds(blk, 1), :])).then_inc(s_c[j], 16)
                        sp.dma_start(as_in[:, j, :], one(logit[:, bass.ds(blk, 1), 0:HEADS])).then_inc(s_c[j], 16)

                    with sp.Fori(0, NCH) as c:
                        t = g * NCH + c
                        sp.wait_ge(s_gpv, t * NB + RING)
                        for j in range(RING):
                            load(c, j, j)
                        with sp.Fori(1, NB // RING) as i:
                            for j in range(RING):
                                sp.wait_ge(s_rm, t * MAXOPS + 1 + (1 + HEADS) * (i * RING + j - RING + 1))
                                load(c, i * RING + j, j)
                        sp.wait_ge(s_rm, (t + 1) * MAXOPS)
                        stand(sp)
                        with sp.Fori(0, NB // RING) as i:
                            for j in range(RING):
                                sp.wait_ge(s_gpv, t * NB + i * RING + j + 1)
                                load(c, i * RING + j, j)
                with sp.Else():
                    counts16_v = counts16.rearrange("(b p) f -> b p f", p=P)
                    with sp.Fori(0, NFC) as c:
                        with sp.Fori(0, NFC) as i:
                            for j in range(RING):
                                n = (f * NFC + c) * NB + i * RING + j
                                sp.wait_ge(s_head, HEADS * n + HEADS)
                                sp.dma_start(c16[:, j, :], counts16_v[bass.ds(i * RING + j, 1), :, bass.ds(c * FC, FC)]
                                             .rearrange("b p f -> p (b f)")).then_inc(s_fc[j], 16)
            sp.wait_ge(s_fin, 1)
            sp.dma_start(out[0:(NB - 1) * P, :].rearrange("(b p) d -> p b d", p=P), y_sb[:, 0:NB - 1, :]).then_inc(s_out, 16)
            sp.dma_start(out[(NB - 1) * P:N, :], y_sb[0:TAIL, NB - 1, :]).then_inc(s_out, 16)
            sp.wait_ge(s_out, 32)

        @block.gpsimd
        def _(pool):
            nc.gpsimd.memset(ones[:], 1.0).then_inc(s_pool0, 1)
            nc.gpsimd.memset(den_sel[:], 0.0).then_inc(s_pool0, 1)
            pool.wait_ge(s_pool0, 2)
            nc.gpsimd.affine_select(out=ident[:], in_=ones[:], compare_op=ALU.is_equal, fill=0.0, base=0,
                                    pattern=[[-1, P]], channel_multiplier=1).then_inc(s_pool0, 1)
            nc.gpsimd.affine_select(out=heads(den_sel[:]), in_=heads(den_sel[:]), compare_op=ALU.not_equal, fill=1.0,
                                    base=-DH, pattern=[[-HS, HEADS], [0, HS]], channel_multiplier=1).then_inc(s_pool0, 1)
            nc.gpsimd.affine_select(out=lower[:], in_=ones[0:EP, 0:EP], compare_op=ALU.is_gt, fill=0.0, base=0,
                                    pattern=[[-1, EP]], channel_multiplier=1).then_inc(s_pool0, 1)
            nc.gpsimd.affine_select(out=ident16[:], in_=ones[:], compare_op=ALU.is_equal, fill=0.0, base=0,
                                    pattern=[[-1, P]], channel_multiplier=1).then_inc(s_pool0, 1)
            nc.gpsimd.iota(dump_i[:], [[0, 1]], base=CELLS, channel_multiplier=1).then_inc(s_pool0, 1)

            pool.sem_inc(s_amax, 1)
            pool.sem_inc(s_comb, 1)

            def scatter_set(g, slot, into):
                pool.wait_ge(s_cell, g + 1)
                for k, (q, before) in enumerate(into):
                    if not isinstance(before, int) or before > 0:
                        pool.wait_ge(s_scat[q], 16 * before)
                    stand(pool)
                    nc.gpsimd.indirect_dma_start(plane[q], bass.IndirectOffsetOnAxis(cell[:, slot, k:k + 1], 0),
                                                 addend[:, slot, k:k + 1], None, compute_op=ALU.add).then_inc(s_scat[q], 16)
                pool.sem_inc(s_landed, 1)

            def cleared(q):
                for u in range(2):
                    pool.wait_ge(s_zero[q][u], 16 * ((ZN + 1 - u) // 2))

            pool.sem_inc(s_landed, 3)
            order = [q for planes in range(1, PLANES) for r in range(EARLY) for q in range(planes)]
            for g in range(EARLY_SETS):
                into = []
                for t in range(g * SET, (g + 1) * SET):
                    q, before = order[t], order[:t].count(order[t])
                    if before == 0:
                        cleared(q)
                    into.append((q, before))
                scatter_set(g, g % 4, into)
            cleared(PLANES - 1)
            scatter_set(EARLY_SETS, 0, [(q, INTO[q] - (SETS - EARLY_SETS)) for q in range(PLANES)])
            for g in range(1, 4):
                scatter_set(EARLY_SETS + g, g, [(q, INTO[q] - (SETS - EARLY_SETS) + g) for q in range(PLANES)])
            with pool.Fori(EARLY_SETS // 4 + 1, SETS // 4) as i:
                for slot in range(4):
                    g = i * 4 + slot
                    scatter_set(g, slot, [(q, g + (INTO[q] - SETS)) for q in range(PLANES)])

            with pool.Fori(0, STEPS // RING) as i:
                for j in range(RING):
                    n = i * RING + j
                    for h in range(CLIPPED):
                        pool.wait_ge(s_cnt, n + 1 + RING)
                        pool.wait_ge(s_exp, n * HEADS + h + 1)
                        stand(pool)
                        w = wts[:, (j * HEADS + h) % UR, :]
                        nc.gpsimd.tensor_tensor(w, w, cnt[:, j, :], ALU.mult).then_inc(s_w, 1)
            with pool.Fori(0, LAYERS) as l:
                pool.wait_ge(s_ext, l + 1)
                stand(pool)
                nc.gpsimd.partition_all_reduce(extremes[:], extreme[:], P, RMAX).then_inc(s_ar, 1)
                pool.wait_ge(s_route, l + 1)
                stand(pool)
                general = pool.value_load(route[0:1, 0:1], min_val=0, max_val=1)
                g = pool.value_load(route[0:1, 1:2], min_val=0, max_val=LAYERS)
                f = pool.value_load(route[0:1, 2:3], min_val=0, max_val=LAYERS)
                with pool.If(general == 1):
                    with pool.Fori(0, NCH) as c:
                        pool.wait_ge(s_rm, (g * NCH + c + 1) * MAXOPS)
                        stand(pool)
                        nc.gpsimd.partition_all_reduce(all_max, run_max, P, RMAX).then_inc(s_amax, 1)
                with pool.Else():
                    W = DH + 1
                    s4 = sums[:, :, 0:HEADS * 4 * W].rearrange("p d (h f) -> p d h f", h=HEADS)
                    both, low = s4[:, :, :, 0:2 * W], s4[:, :, :, W:2 * W]

                    def mask(t, i, j):
                        n = (t * (NB // RING) + i) * RING + j
                        pool.wait_ge(s_sign, 2 * n + 2)
                        pool.wait_ge(s_fc[j], 16 * (t * (NB // RING) + i + 1))
                        stand(pool)
                        o = chosen[:, (j * HEADS + HEADS - 1) % UR, :]
                        nc.gpsimd.tensor_tensor(o, o, c16[:, j, :], ALU.mult).then_inc(s_chlast, 1)

                    def combine(c, k):
                        t = f * NFC + c
                        if k == 0:
                            pool.wait_ge(s_fsum, (t + 1) * FB + 1)
                        else:
                            pool.wait_ge(s_comb, 4 * t + k + 1)
                        stand(pool)
                        if k == 0:
                            last = nc.gpsimd.tensor_tensor(both, both, s4[:, :, :, 2 * W:4 * W], ALU.add)
                        elif k == 1:
                            last = nc.gpsimd.tensor_tensor(
                                low, sums[:, :, HEADS * 4 * W:HEADS * 5 * W].rearrange("p d (h f) -> p d h f", h=HEADS),
                                low, ALU.subtract)
                        elif k == 2:
                            for b in range(2):
                                v = s4[:, :, :, b * W:(b + 1) * W]
                                last = nc.gpsimd.tensor_tensor(v, v, scale_d[:, b, bass.ds(c * FB, FB), :].unsqueeze(3)
                                                               .to_broadcast([P, FB, HEADS, W]), ALU.mult)
                        else:
                            last = nc.gpsimd.tensor_tensor(total[:, bass.ds(c * FB, FB), :, :], s4[:, :, :, 0:W], low, ALU.add)
                        last.then_inc(s_comb, 1)

                    def chunk(c, before):
                        t = f * NFC + c
                        for j in range(RING):
                            mask(t, 0, j)
                            if before and j >= 1:
                                combine(c - 1, j - 1)
                        with pool.Fori(1, NB // RING) as i:
                            for j in range(RING):
                                mask(t, i, j)

                    chunk(0, False)
                    with pool.Fori(1, NFC) as c:
                        chunk(c, True)
                    for k in range(4):
                        combine(NFC - 1, k)

        @block.tensor
        def _(pe):
            pe.sem_inc(s_pv, HEADS * RING)
            pe.sem_inc(s_tr, RING)
            pe.sem_inc(s_rtr, 1)
            pe.sem_inc(s_gpv, RING)
            pe.sem_inc(s_keyrow, 2)
            pe.sem_inc(s_head, HEADS * RING)
            pe.sem_inc(s_qk, HEADS * RING)
            pe.wait_ge(s_x, 80)
            pe.wait_ge(s_pool0, 7)
            m = 0

            def bank(m):
                if m >= 2:
                    pe.wait_ge(s_pe, m - 1)
                return psP[:, m % 2, :]

            for _, g, k in G4:
                ps = bank(m)
                for b in range(k):
                    last = nc.tensor.transpose(ps[0:D, b * P:(b + 1) * P], x_sb[:, g + b, :], ident[:])
                last.then_inc(s_pm, 1)
                m += 1
            pe.wait_ge(s_pe, m)
            for _, g, k in G4:
                ps = bank(m)
                for b in range(k):
                    last = nc.tensor.matmul(ps[:, b * P:(b + 1) * P], featT[0:D, (g + b) * P:(g + b + 1) * P],
                                            w_pad[0:D, 2, :], start=True, stop=True)
                last.then_inc(s_pm, 1)
                m += 1
            for t in range(2):
                with pe.Fori(0, NA // 4) as i:
                    for u in range(4):
                        pe.wait_ge(s_rest, t * NA + i * 4 + u + 1)
                        nc.tensor.matmul(psS[:, u, 0:AW], w_pad[0:D, t, :], featT[0:D, bass.ds((i * 4 + u) * AW, AW)],
                                         start=True, stop=True).then_inc(s_proj, 1)

            with pe.Fori(0, SETS // 2) as i:
                for u in range(2):
                    pe.wait_ge(s_diag, i * 2 + u + 1)
                    pe.wait_ge(s_same, i * 2 + u + 1)
                    nc.tensor.matmul(psK[u][0:EP, 0:SET * EP], ones[0:EP, 0:EP], diag[:, u, :],
                                     start=True, stop=True).then_inc(s_keyrow, 1)

            def scores(c, n, j, h, k):
                if h == 0:
                    pe.wait_ge(s_kv[j], 32 * (k + 1))
                if (h - 2) % HEADS == HEADS - 1:
                    pe.wait_ge(s_read, n + 1)
                else:
                    pe.wait_ge(s_clip, CLIPPED * n + (CLIPPED, 0, CLIPPED + 1, CLIPPED + 2)[h])
                for half in range(2):
                    for t, q in enumerate((q_first, q_second)):
                        last = nc.tensor.matmul(psU[h % 2][:, half, :], k_in[:, j, t, h, :],
                                                q[:, h, bass.ds(c * FC + half * (FC // 2), FC // 2)],
                                                start=(t == 0), stop=(t == 1))
                last.then_inc(s_qk, 1)

            def transposes(n, j):
                pe.wait_ge(s_c16, n + 1)
                pe.wait_ge(s_trev, n + 1)
                for d in range(FB):
                    last = nc.tensor.transpose(psT[:, d * P:(d + 1) * P], cnt16[:, j, d * P:(d + 1) * P], ident16[:])
                last.then_inc(s_tr, 1)

            def sums(n, j, h):
                if h == HEADS - 1:
                    pe.wait_ge(s_wlast, n + 1)
                else:
                    pe.wait_ge(s_w, CLIPPED * n + h + 1)
                for half in range(2):
                    last = nc.tensor.matmul(psV[HS * h:HS * h + HS, half, :], v_in[:, j, HS * h:HS * h + HS],
                                            wts[:, (j * HEADS + h) % UR, half * (FC // 2):(half + 1) * (FC // 2)],
                                            start=False, stop=False, skip_group_check=True)
                last.then_inc(s_pv, 1)

            def clear_sums():
                nc.tensor.matmul(psO[:, 0:CH], zero16[:, 0:P], zero16[:, 0:CH],
                                 start=True, stop=False, skip_group_check=True)

            def step(c, i, j, last):
                n = c * NB + i * RING + j
                for h in range(HEADS):
                    more, hh = divmod(h + SKEW, HEADS)
                    if not (last and j + more >= RING):
                        scores(c + (j + more) // RING if isinstance(i, int) else c, n + more, (j + more) % RING, hh,
                               c * (NB // RING) + i + (j + more) // RING)
                    if h == 0:
                        transposes(n, j)
                    sums(n, j, h)

            def chunk(c, last):
                pe.wait_ge(s_tot, c + 1)
                for half in range(2):
                    nc.tensor.matmul(psV[:, half, :], zero16[:, 0:P], zero16[:, 0:FC // 2], start=True, stop=False,
                                     skip_group_check=True)
                with pe.Fori(0, NB // RING - 1) as i:
                    for j in range(RING):
                        step(c, i, j, False)
                for j in range(RING):
                    step(c, NB // RING - 1, j, last)

            pe.wait_ge(s_qc, 32)
            for u in range(SKEW):
                scores(0, u // HEADS, u // HEADS, u % HEADS, 0)
            with pe.Fori(0, NFC - 1) as c:
                chunk(c, False)
            chunk(NFC - 1, True)

            pe.wait_ge(s_tot, NFC + 1)
            for m, g, k in G4:
                if m >= 2:
                    pe.wait_ge(s_b1e, m - 1)
                for b in range(k):
                    last = nc.tensor.transpose(psP[:, m % 2, b * P:(b + 1) * P], outT[:, (g + b) * P:(g + b + 1) * P], ident[:])
                last.then_inc(s_b1, 1)

            pe.wait_ge(s_x1, 1)
            for m, g, k in G4:
                if m >= 2:
                    pe.wait_ge(s_b2e, m - 1)
                for b in range(k):
                    last = nc.tensor.transpose(psP[:, m % 2, b * P:(b + 1) * P], x1[:, g + b, :], ident[:])
                last.then_inc(s_b2, 1)
            pe.wait_ge(s_b2e, len(G4))

            with pe.Fori(0, LAYERS) as l:
                pe.wait_ge(s_layer, l + 1)
                pe.wait_ge(s_lw, (l + 1) * 16 * 4 * HEADS)
                nc.tensor.transpose(psP[:, 0, 0:P], w_gat[:], ident[:]).then_inc(s_lp, 1)
                pe.wait_ge(s_lpe, l * LPREP + 1)
                nc.tensor.matmul(psP[:, 1, 0:2 * HEADS], w_gatT[:], att_blk[:], start=True, stop=True).then_inc(s_lp, 1)
                pe.wait_ge(s_lpe, l * LPREP + 2)
                for m, g, k in G3:
                    if m >= 2:
                        pe.wait_ge(s_lpe, l * LPREP + 2 + 2 * (m - 1))
                    for b in range(k):
                        last = nc.tensor.matmul(psP[:, m % 2, b * HC:(b + 1) * HC], featT[:, (g + b) * P:(g + b + 1) * P],
                                                w_cat[:], start=True, stop=True)
                    last.then_inc(s_lp, 1)
                pe.wait_ge(s_wad, l + 1)
                stand(pe)
                with pe.Fori(0, NR // AW) as i:
                    for h in range(HEADS):
                        pe.wait_ge(s_adre, (l * (NR // AW) + i) * HEADS + h + 1)
                        nc.tensor.matmul(psS[:, h, 0:AW], wad[:, h, :], featT[:, bass.ds(i * AW, AW)],
                                         start=True, stop=True).then_inc(s_adr, 1)
                pe.wait_ge(s_adre, (l + 1) * (NR // AW) * HEADS + HEADS)
                pe.wait_ge(s_route, l + 1)
                stand(pe)
                general = pe.value_load(route[0:1, 0:1], min_val=0, max_val=1)
                g = pe.value_load(route[0:1, 1:2], min_val=0, max_val=LAYERS)
                f = pe.value_load(route[0:1, 2:3], min_val=0, max_val=LAYERS)
                with pe.If(general == 1):
                    with pe.Fori(0, NFC) as c:
                        with pe.Fori(0, NB) as b:
                            m = g * STEPS + c * NB + b
                            pe.wait_ge(s_rsum, m + 2)
                            pe.wait_ge(s_rev, m + 1)
                            for d in range(FB):
                                last = nc.tensor.transpose(acc[:, d // 4, (d % 4) * P:(d % 4 + 1) * P],
                                                           r_cnt[:, d * P:(d + 1) * P], ident[:])
                            last.then_inc(s_rtr, 1)
                    pe.wait_ge(s_rev, (g + 1) * STEPS + 1)
                    stand(pe)
                    with pe.Fori(0, NCH) as c:
                        t = g * NCH + c
                        pe.wait_ge(s_num, t + 1)
                        for h in range(HEADS):
                            last = nc.tensor.matmul(psS[:, h, 0:CH], wad[:, h, :], featT[:, bass.ds(c * CH, CH)],
                                                    start=True, stop=True)
                        last.then_inc(s_ad, 1)
                        clear_sums()
                        with pe.Fori(0, NB // RING) as i:
                            for j in range(RING):
                                pe.wait_ge(s_gw, t * NB + i * RING + j + 1)
                                for h in range(HEADS):
                                    last = nc.tensor.matmul(psO[HS * h:HS * h + HS, 0:CH], h_in[:, j, HS * h:HS * h + HS],
                                                            g_wts[:, j, h * CH:(h + 1) * CH],
                                                            start=False, stop=False, skip_group_check=True)
                                last.then_inc(s_gpv, 1)
                        pe.wait_ge(s_num, t + 2)
                        nc.tensor.matmul(psD[:, 0:CH], den_sel[:], g_num[:], start=True, stop=True).then_inc(s_den, 1)
                with pe.Else():
                    pe.wait_ge(s_part, (f + 1) * 4)
                    pe.wait_ge(s_low, (f + 1) * 2)
                    stand(pe)
                    W = DH + 1
                    with pe.Fori(0, NFC) as c:
                        t = f * NFC + c
                        pe.wait_ge(s_fsum, t * FB + 1)
                        for d in range(FB):
                            nc.tensor.matmul(acc[:, d, 0:500], zero16[:, 0:P], zero16[:, 0:500], start=True, stop=False,
                                             skip_group_check=True)
                        with pe.Fori(0, NB // RING) as i:
                            for j in range(RING):
                                n = t * NB + i * RING + j
                                blk = i * RING + j
                                pe.wait_ge(s_fc[j], 16 * (t * (NB // RING) + i + 1))
                                quad = parts[:, bass.ds(blk * HEADS, HEADS), :, W:2 * W]
                                for d in range(FB):
                                    for k in range(3):
                                        nc.tensor.matmul(acc[:, d, HEADS * 4 * W:HEADS * 5 * W], c16[:, j, d * P:(d + 1) * P],
                                                         quad[:, :, k, :], start=False, stop=False, skip_group_check=True)
                                for h in range(HEADS):
                                    if h < HEADS - 1:
                                        pe.wait_ge(s_chosen, (HEADS - 1) * n + h + 1)
                                    else:
                                        pe.wait_ge(s_chlast, n + 1)
                                    mine = parts[:, bass.ds(blk * HEADS + h, 1), :, :].rearrange("p a k f -> p (a k f)")
                                    for d in range(FB):
                                        w = chosen[:, (j * HEADS + h) % UR, d * P:(d + 1) * P]
                                        nc.tensor.matmul(acc[:, d, h * 4 * W:(h + 1) * 4 * W], w, mine[:, 0:4 * W],
                                                         start=False, stop=False, skip_group_check=True)
                                        last = nc.tensor.matmul(acc[:, d, h * 4 * W:h * 4 * W + 2 * W], w, mine[:, 4 * W:6 * W],
                                                                start=False, stop=False, skip_group_check=True)
                                    last.then_inc(s_head, 1)
                    pe.wait_ge(s_xn, f + 1)
                    for m, gg, k in G4:
                        if m >= 2:
                            pe.wait_ge(s_xte, f * len(G4) + m - 1)
                        for b in range(k):
                            last = nc.tensor.transpose(psP[:, m % 2, b * P:(b + 1) * P], x_next[:, gg + b, :], ident[:])
                        last.then_inc(s_xt, 1)
            pe.wait_ge(s_layer, LAYERS + 1)
            for m, g, k in G4:
                if m >= 2:
                    pe.wait_ge(s_fe, m - 1)
                for b in range(k):
                    last = nc.tensor.transpose(psP[:, m % 2, b * P:(b + 1) * P], featT[:, (g + b) * P:(g + b + 1) * P], ident[:])
                last.then_inc(s_f, 1)

        @block.scalar
        def _(act):
            act.sem_inc(s_read, 1)
            act.sem_inc(s_trev, 1)
            act.sem_inc(s_tot, 1)
            act.sem_inc(s_adre, HEADS)
            act.sem_inc(s_fsum, 1)
            act.sem_inc(s_store, 16)
            act.sem_inc(s_rev, 1)
            act.sem_inc(s_rst, 16)
            act.wait_ge(s_init, 1)
            m = 0
            for _, g, k in G4:
                act.wait_ge(s_pm, m + 1)
                nc.scalar.copy(featT[0:D, g * P:(g + k) * P], psP[0:D, m % 2, 0:k * P]).then_inc(s_pe, 1)
                m += 1
            for _, g, k in G4:
                act.wait_ge(s_pm, m + 1)
                nc.scalar.copy(v_sb[:, g:g + k, :].rearrange("p b (h c) -> p (b h) c", h=HEADS)[:, :, 0:DH],
                               psP[:, m % 2, 0:k * P].rearrange("p (a c) -> p a c", c=HS)[:, :, 0:DH]).then_inc(s_pe, 1)
                m += 1

            for t in range(2):
                with act.Fori(0, NA // 4) as i:
                    for u in range(4):
                        at = bass.ds((i * 4 + u) * AW, AW)
                        m = t * NA + i * 4 + u
                        act.wait_ge(s_proj, m + 1)
                        nc.scalar.copy(piece[:, t, 0, at], psS[:, u, 0:AW]).then_inc(s_first, 1)
                        act.wait_ge(s_rest, m + 5)
                        nc.scalar.copy(piece[:, t, 1, at], rest[:, u % 2, :]).then_inc(s_second, 1)

            act.wait_ge(s_key, 1)
            with act.Fori(0, SETS // 2) as i:
                for u in range(2):
                    act.wait_ge(s_keyrow, i * 2 + u + 1)
                    for q in range(SET):
                        last = nc.scalar.activation(diag[:, u, q * EP:(q + 1) * EP], ident[0:EP, 0:EP], ACT.Copy,
                                                    scale=key[:, bass.ds((i * 2 + u) * SET + q, 1)])
                    last.then_inc(s_diag, 1)

            rows16 = counts16.rearrange("(c d p) n -> c p d n", d=FB, p=P)

            def exps(n, j):
                act.wait_ge(s_cnt, n + 1 + RING)
                nc.scalar.copy(cnt16[:, j, :], cnt[:, j, :]).then_inc(s_c16, 1)
                for h in range(HEADS):
                    w = wts[:, (j * HEADS + h) % UR, :]
                    if h < CLIPPED:
                        act.wait_ge(s_clip, CLIPPED * (n + 1) + h + 1)
                        nc.scalar.activation(w, w, ACT.Exp).then_inc(s_exp, 1)
                    else:
                        act.wait_ge(s_pv, HEADS * (n + RING) + h + 1 - UR)
                        act.wait_ge(s_qk, HEADS * (n + RING) + h + 1)
                        nc.scalar.activation(w.rearrange("p (k f) -> p k f", k=2), psU[h % 2], ACT.Relu, bias=plus10[:]
                                             ).then_inc(s_read, 1)
                        act.wait_ge(s_read, n + 2)
                        nc.scalar.activation(w, w, ACT.Exp, bias=minus10[:]).then_inc(s_exp, 1)

            def turned(c, i, j):
                k = c * (NB // RING) + i
                act.wait_ge(s_tr, k * RING + j + 1 + RING)
                if j == 0:
                    act.wait_ge(s_store, 16 * (k + 1))
                nc.scalar.copy(cntT[:, :, j * P:(j + 1) * P], psT[:, 0:FC].rearrange("p (d f) -> p d f", d=FB)).then_inc(s_trev, 1)
                if j == RING - 1:
                    act.wait_ge(s_trev, (k + 1) * RING + 1)
                    act.dma_start(rows16[bass.ds(c, 1), :, :, bass.ds(i * RING * P, RING * P)].rearrange("c p d n -> p (c d) n"),
                                  cntT[:]).then_inc(s_store, 16)

            def chunk_sums(c):
                act.wait_ge(s_pv, HEADS * (NB * (c + 1) + RING))
                nc.scalar.copy(outT[:, bass.ds(c * FC, FC)].rearrange("p (k f) -> p k f", k=2), psV).then_inc(s_tot, 1)

            exps(0, 0)
            turned(0, 0, 0)

            def chunk(c, last):
                with act.Fori(0, NB // RING - 1) as i:
                    for jj in range(RING):
                        j = (jj + 1) % RING
                        exps(c * NB + i * RING + jj + 1, j)
                        turned(c, i + (jj + 1) // RING, j)
                for j in range(1, RING):
                    exps(c * NB + NB - RING + j, j)
                    turned(c, NB // RING - 1, j)
                if not last:
                    exps((c + 1) * NB, 0)
                chunk_sums(c)
                if not last:
                    turned(c + 1, 0, 0)

            with act.Fori(0, NFC - 1) as c:
                chunk(c, False)
            chunk(NFC - 1, True)
            for m, g, k in G4:
                act.wait_ge(s_b1, m + 1)
                nc.scalar.copy(sums0[:, g:g + k, :], psP[:, m % 2, 0:k * P].rearrange("p (b f) -> p b f", b=k)).then_inc(s_b1e, 1)
            act.wait_ge(s_var, 1)
            nc.scalar.activation(stat[:, 2, :], stat[:, 1, :], ACT.Sqrt, bias=eps[:], scale=1.0 / D).then_inc(s_std, 1)
            for m, g, k in G4:
                act.wait_ge(s_b2, m + 1)
                nc.scalar.copy(featT[:, g * P:(g + k) * P], psP[:, m % 2, 0:k * P]).then_inc(s_b2e, 1)

            with act.Fori(0, LAYERS) as l:
                act.wait_ge(s_lp, l * (2 + len(G3)) + 1)
                nc.scalar.copy(w_gatT[:], psP[:, 0, 0:P]).then_inc(s_lpe, 1)
                act.wait_ge(s_lw, (l + 1) * 16 * 4 * HEADS)
                nc.scalar.copy(w_cat[:, 0:P], w_gat[:])
                act.wait_ge(s_lp, l * (2 + len(G3)) + 2)
                nc.scalar.copy(w_cat[:, P:HC], psP[:, 1, 0:2 * HEADS]).then_inc(s_lpe, 1)
                for m, g, k in G3:
                    act.wait_ge(s_lp, l * (2 + len(G3)) + 3 + m)
                    ps = psP[:, m % 2, 0:k * HC].rearrange("p (b f) -> p b f", b=k)
                    nc.scalar.copy(h_sb[:, g:g + k, :].rearrange("p b (h c) -> p b h c", h=HEADS)[:, :, :, 0:DH],
                                   ps[:, :, 0:P].rearrange("p b (h c) -> p b h c", h=HEADS)[:, :, :, 0:DH]).then_inc(s_lpe, 1)
                    nc.scalar.copy(logit[:, g:g + k, :], ps[:, :, P:HC]).then_inc(s_lpe, 1)
                with act.Fori(0, NR // AW) as i:
                    for h in range(HEADS):
                        act.wait_ge(s_adr, (l * (NR // AW) + i) * HEADS + h + 1)
                        nc.scalar.copy(ad_row[:, h, bass.ds(i * AW, AW)], psS[:, h, 0:AW]).then_inc(s_adre, 1)
                act.wait_ge(s_route, l + 1)
                stand(act)
                general = act.value_load(route[0:1, 0:1], min_val=0, max_val=1)
                g = act.value_load(route[0:1, 1:2], min_val=0, max_val=LAYERS)
                f = act.value_load(route[0:1, 2:3], min_val=0, max_val=LAYERS)
                with act.If(general == 1):
                    rows32 = counts.rearrange("(c d p) n -> c p d n", d=FB, p=P)
                    with act.Fori(0, NFC) as c:
                        with act.Fori(0, NB) as b:
                            m = g * STEPS + c * NB + b
                            act.wait_ge(s_rtr, m + 2)
                            act.wait_ge(s_rst, 16 * (m + 1))
                            nc.scalar.copy(r_out[:, 0:512], acc[:, 0, :])
                            nc.scalar.copy(r_out[:, 512:FC], acc[:, 1, 0:FC - 512]).then_inc(s_rev, 1)
                            act.wait_ge(s_rev, m + 2)
                            act.dma_start(rows32[bass.ds(c, 1), :, :, bass.ds(b * P, P)].rearrange("c p d n -> p (c d) n"),
                                          r_out[:].rearrange("p (d f) -> p d f", d=FB)).then_inc(s_rst, 16)
                    with act.Fori(0, NCH) as c:
                        t = g * NCH + c
                        act.wait_ge(s_ad, t + 1)
                        act.wait_ge(s_m, 4 * t + 1)
                        with act.Fori(0, NB // RING) as i:
                            for j in range(RING):
                                n = t * NB + i * RING + j
                                act.wait_ge(s_c[j], 48 * (2 * t * (NB // RING) + NB // RING + i + 1))
                                act.wait_ge(s_gpv, n + 1)
                                for h in range(HEADS):
                                    last = nc.scalar.activation(g_wts[:, j, h * CH:(h + 1) * CH], psS[:, h, 0:CH],
                                                                ACT.Identity, bias=as_in[:, j, h:h + 1])
                                last.then_inc(s_z, 1)
                                act.wait_ge(s_zm, 2 * n + 2)
                                nc.scalar.activation(g_wts[:, j, :], g_wts[:, j, :], ACT.Exp).then_inc(s_ez, 1)
                with act.Else():
                    act.wait_ge(s_sc, 2 * f + 1)
                    for k, scale in enumerate((1.0, 0.2)):
                        last = nc.scalar.activation(scale_s[:, :, :, k], neg_as[:], ACT.Exp, scale=-scale)
                    last.then_inc(s_sce, 1)
                    act.wait_ge(s_sc, 2 * f + 2)
                    nc.scalar.activation(scale_d[:], scale_d[:], ACT.Exp).then_inc(s_sce, 1)
                    for k in range(2):
                        for half in range(2):
                            act.wait_ge(s_term, 4 * f + 2 * k + half + 1)
                            a = slice(half * NB * HEADS // 2, (half + 1) * NB * HEADS // 2)
                            nc.scalar.copy(parts[:, a, k, :], terms[:, a, :]).then_inc(s_part, 1)
                    act.wait_ge(s_adre, (l + 1) * (NR // AW) * HEADS + HEADS)

                    def sign(n, c, blk, j):
                        h = HEADS - 1
                        o = chosen[:, (j * HEADS + h) % UR, :]
                        act.wait_ge(s_head, HEADS * (n + RING) + h + 1 - UR)
                        stand(act)
                        nc.scalar.activation(o, ad_row[:, h, bass.ds(c * FC, FC)], ACT.Sign,
                                             bias=one(logit[:, bass.ds(blk, 1), h:h + 1])).then_inc(s_sign, 1)
                        act.wait_ge(s_sign, 2 * n + 1)
                        nc.scalar.activation(o, o, ACT.Relu).then_inc(s_sign, 1)

                    def chunk_sums(t):
                        act.wait_ge(s_head, HEADS * ((t + 1) * NB + RING))
                        act.wait_ge(s_comb, 4 * t + 1)
                        for d in range(FB):
                            nc.scalar.copy(sums[:, d, :], acc[:, d, 0:500]).then_inc(s_fsum, 1)

                    def chunk(c, last):
                        t = f * NFC + c
                        with act.Fori(0, NB // RING - 1) as i:
                            for jj in range(RING):
                                sign(t * NB + i * RING + jj + 1, c, i * RING + jj + 1, (jj + 1) % RING)
                        for j in range(1, RING):
                            sign(t * NB + NB - RING + j, c, NB - RING + j, j)
                        if not last:
                            sign((t + 1) * NB, c + 1, 0, 0)
                        chunk_sums(t)

                    sign(f * NFC * NB, 0, 0, 0)
                    with act.Fori(0, NFC - 1) as c:
                        chunk(c, False)
                    chunk(NFC - 1, True)
                    for m, gg, k in G4:
                        act.wait_ge(s_xt, f * len(G4) + m + 1)
                        nc.scalar.activation(featT[:, gg * P:(gg + k) * P], psP[:, m % 2, 0:k * P], ACT.Relu, bias=bias[:]
                                             ).then_inc(s_xte, 1)
            act.wait_ge(s_var, 2)
            nc.scalar.activation(stat[:, 2, :], stat[:, 1, :], ACT.Sqrt, bias=eps[:], scale=1.0 / D).then_inc(s_std, 1)

        @block.vector
        def _(dve):
            steps = [0]

            def link(ins):
                steps[0] += 1
                ins.then_inc(s_chain, 1)
                dve.wait_ge(s_chain, steps[0])

            dve.sem_inc(s_cnt, RING)
            dve.sem_inc(s_clip, CLIPPED)
            dve.sem_inc(s_rest, 4)
            dve.sem_inc(s_rsum, 1)
            dve.sem_inc(s_same, 2)
            dve.sem_inc(s_num, 1)
            dve.sem_inc(s_layer, 1)
            nc.vector.memset(x_sb[:], 0.0)
            nc.vector.memset(w_pad[:], 0.0)
            nc.vector.memset(w_gat[:], 0.0)
            nc.vector.memset(att_blk[:], 0.0)
            nc.vector.memset(bias[:], 0.0)
            nc.vector.memset(eps[:], 1e-5)
            nc.vector.memset(minus10[:], -10.0)
            nc.vector.memset(plus10[:], 10.0)
            nc.vector.memset(zeros[:], 0)
            nc.vector.memset(zero16[:], 0.0)
            nc.vector.memset(step_max[:], 0.0)
            nc.vector.memset(route_f[:], 0.0)
            link(nc.vector.memset(v_sb[:], 0.0))
            nc.vector.memset(v_sb[:].rearrange("p b (h c) -> p (b h) c", h=HEADS)[:, :, DH:DH + 1], 1.0).then_inc(s_init, 1)
            dve.wait_ge(s_edges, 32)
            dve.wait_ge(s_pool0, 7)
            link(nc.vector.tensor_copy(dump[:], dump_i[:]))
            link(nc.vector.scalar_tensor_tensor(key[:], dst_sb[:], float(NR), src_sb[:], ALU.mult, ALU.add))
            nc.vector.tensor_scalar(keyd[:], key[:], dump[:, 0:1], None, ALU.subtract).then_inc(s_key, 1)
            dve.wait_ge(s_key, 1)

            for t in range(2):
                with dve.Fori(0, NA // 4) as i:
                    for u in range(4):
                        at = bass.ds((i * 4 + u) * AW, AW)
                        m = t * NA + i * 4 + u
                        dve.wait_ge(s_first, m + 1)
                        nc.vector.tensor_tensor(rest[:, u % 2, :], psS[:, u, 0:AW], piece[:, t, 0, at], ALU.subtract
                                                ).then_inc(s_rest, 1)
                        dve.wait_ge(s_second, m + 1)
                        nc.vector.tensor_tensor(piece[:, t, 2, at], rest[:, u % 2, :], piece[:, t, 1, at], ALU.subtract
                                                ).then_inc(s_piece, 1)

            NDUP = 8
            with dve.Fori(0, SETS // 4) as ii:
                for half in range(2):
                    i = ii * 2 + half

                    def after(k):
                        dve.wait_ge(s_dup, i * NDUP + k)

                    def sets(ap):
                        return ap.rearrange("p (q e) -> p q e", q=SET)
                    kq = [bass.ds((i * 2 + u) * SET, SET) for u in range(2)]
                    for u in range(2):
                        dve.wait_ge(s_keyrow, i * 2 + u + 3)
                        nc.vector.tensor_tensor(sets(same[:, u, :]), sets(psK[u][0:EP, 0:SET * EP]),
                                                key[:, kq[u]].unsqueeze(2).to_broadcast([EP, SET, EP]), ALU.is_equal).then_inc(s_same, 1)
                    for u in range(2):
                        dve.wait_ge(s_same, i * 2 + u + 3)
                        nc.vector.tensor_tensor(sets(earlier[:, u, :]), sets(same[:, u, :]),
                                                lower[:].unsqueeze(1).to_broadcast([EP, SET, EP]), ALU.mult).then_inc(s_dup, 1)
                    for u in range(2):
                        after(u + 1)
                        nc.vector.tensor_reduce(n_earlier[:, u, :], sets(earlier[:, u, :]), AX_X, ALU.add).then_inc(s_dup, 1)
                    for u in range(2):
                        dve.wait_ge(s_landed, i * 2 + u + 1)
                        with nc.allow_low_precision("whole numbers up to 125"):
                            nc.vector.tensor_reduce(addend[:, half * 2 + u, :], sets(same[:, u, :]), AX_X, ALU.add).then_inc(s_dup, 1)
                    for u in range(2):
                        after(u + 3)
                        nc.vector.scalar_tensor_tensor(kfirst[:, u, :], n_earlier[:, u, :], 0.0, keyd[:, kq[u]],
                                                       ALU.is_equal, ALU.mult).then_inc(s_dup, 1)
                    for u in range(2):
                        after(u + 7)
                        nc.vector.tensor_scalar(cell[:, half * 2 + u, :], kfirst[:, u, :], dump[:, 0:1], None, ALU.add).then_inc(s_cell, 1)

            dve.wait_ge(s_pe, len(G4))
            link(nc.vector.tensor_tensor(x_sb[:], x_sb[:], x_sb[:], ALU.add))

            def epilogue(c_now, floor, pv_done, num, den):
                dve.wait_ge(*pv_done)
                nc.vector.tensor_copy(num[:], psO[:, 0:CH]).then_inc(s_num, 1)
                dve.wait_ge(s_den, c_now + 1)
                nc.vector.tensor_scalar(den[:], psD[:, 0:CH], floor, None, ALU.add).then_inc(s_ep, 1)
                dve.wait_ge(s_ep, c_now * 3 + 1)
                nc.vector.reciprocal(den[:], den[:]).then_inc(s_ep, 1)
                dve.wait_ge(s_ep, c_now * 3 + 2)

            def pair(n, k, j, q):
                if q == 0:
                    dve.wait_ge(s_plane[j], 16 * PLANES * (k + 1))
                nc.vector.tensor_tensor(pl_in[:, j, q, :], pl_in[:, j, q, :], pl_in[:, j, q + 1, :], ALU.add).then_inc(s_pair, 1)

            def count(n, j):
                dve.wait_ge(s_pair, 2 * n + 2)
                dve.wait_ge(s_tr, n + 1)
                stand(dve)
                nc.vector.tensor_tensor_reduce(cnt[:, j, :], pl_in[:, j, 0, :], pl_in[:, j, 2, :], 1.0,
                                               step_max[:, j:j + 1], ALU.add, ALU.max, step_max[:, j:j + 1]).then_inc(s_cnt, 1)

            def clip(n, j, h):
                dve.wait_ge(s_pv, HEADS * (n + RING) + h + 1 - UR)
                dve.wait_ge(s_qk, HEADS * (n + RING) + h + 1)
                nc.vector.tensor_scalar(wts[:, (j * HEADS + h) % UR, :].rearrange("p (k f) -> p k f", k=2), psU[h % 2],
                                        10.0, -10.0, ALU.min, ALU.max).then_inc(s_clip, 1)

            def last_head(n, j):
                dve.wait_ge(s_exp, HEADS * (n + 1))
                dve.wait_ge(s_cnt, n + 1 + RING)
                w = wts[:, (j * HEADS + HEADS - 1) % UR, :]
                nc.vector.scalar_tensor_tensor(w, w, E_HI, cnt[:, j, :], ALU.min, ALU.mult).then_inc(s_wlast, 1)

            def step(n, k, j, more):
                jj, kk = (j + 1) % RING, k + (j + 1) // RING
                if more:
                    clip(n + 1, jj, 0)
                    pair(n + 1, kk, jj, 0)
                    pair(n + 1, kk, jj, 2)
                    clip(n + 1, jj, 1)
                    count(n + 1, jj)
                last_head(n, j)
                if more:
                    clip(n + 1, jj, 2)

            for q in (0, 2):
                pair(0, 0, 0, q)
            for h in range(CLIPPED):
                clip(0, 0, h)
            count(0, 0)

            def chunk(c, last):
                with dve.Fori(0, NB // RING - last) as i:
                    for j in range(RING):
                        step(c * NB + i * RING + j, c * (NB // RING) + i, j, True)
                if last:
                    for j in range(RING):
                        step(STEPS - RING + j, STEPS // RING - 1, j, j < RING - 1)

            with dve.Fori(0, NFC - 1) as c:
                chunk(c, 0)
            chunk(NFC - 1, 1)
            dve.wait_ge(s_b1e, len(G4))
            res = sums0[:].rearrange("p b (h c) -> p b h c", h=HEADS)
            link(nc.vector.tensor_scalar(rden[:], res[:, :, :, DH:DH + 1].rearrange("p b h o -> p b (h o)"), 1e-8, None, ALU.add))
            link(nc.vector.reciprocal(rden[:], rden[:]))
            link(nc.vector.tensor_tensor(res[:, :, :, 0:DH], res[:, :, :, 0:DH],
                                         rden[:].unsqueeze(3).to_broadcast([P, NB, HEADS, DH]), ALU.mult))
            link(nc.vector.memset(res[:, :, :, DH:DH + 1], 1.0))
            x_heads = x_sb[:].rearrange("p b (h c) -> p b h c", h=HEADS)
            link(nc.vector.tensor_tensor(x_heads, x_heads, res[:, :, :, 0:DH], ALU.add))

            def layernorm(n, x_sb):
                link(nc.vector.tensor_reduce(stat[:, 0, :], x_sb, AX_X, ALU.add))
                link(nc.vector.tensor_scalar(stat[:, 0, :], stat[:, 0, :], 1.0 / D, None, ALU.mult))
                link(nc.vector.tensor_tensor(x_sb, x_sb, stat[:, 0, :].unsqueeze(2).to_broadcast([P, NB, D]), ALU.subtract))
                link(nc.vector.tensor_tensor(square, x_sb, x_sb, ALU.mult))
                nc.vector.tensor_reduce(stat[:, 1, :], square, AX_X, ALU.add).then_inc(s_var, 1)
                dve.wait_ge(s_std, n)
                link(nc.vector.reciprocal(stat[:, 3, :], stat[:, 2, :]))

            def wide(ap):
                return ap.rearrange("p b (h c) -> p b h c", h=HEADS)[:, :, :, 0:DH]

            def narrow(ap):
                return ap.rearrange("p b (h c) -> p b h c", h=HEADS)

            link(nc.vector.memset(x1, 0.0))
            layernorm(1, x_sb[:])
            nc.vector.tensor_tensor(wide(x1), narrow(x_sb[:]),
                                    stat[:, 3, :].unsqueeze(2).unsqueeze(3).to_broadcast([P, NB, HEADS, DH]), ALU.mult).then_inc(s_x1, 1)

            link(nc.vector.tensor_reduce(extreme[:, 2 * HEADS:2 * HEADS + 1], step_max[:], AX_X, ALU.max))

            def heads_of(flat):
                return flat.rearrange("p (h f) -> p h f", h=HEADS)

            with dve.Fori(0, LAYERS) as l:
                dve.wait_ge(s_lpe, l * LPREP + 2)
                for h in range(HEADS):
                    last = nc.vector.tensor_scalar(wad[:, h, :], ones[:], w_cat[:, P + HEADS + h:P + HEADS + h + 1], None, ALU.mult)
                last.then_inc(s_wad, 1)
                dve.wait_ge(s_lpe, (l + 1) * LPREP)
                nc.vector.tensor_scalar(neg_as[:], logit[:, :, 0:HEADS], -1.0, None, ALU.mult).then_inc(s_lay, 1)
                nc.vector.tensor_reduce(extreme[:, 0:HEADS], logit[:, :, 0:HEADS].rearrange("p b h -> p h b"), AX_X, ALU.max
                                        ).then_inc(s_lay, 1)
                dve.wait_ge(s_lay, 6 * l + 2)
                nc.vector.tensor_reduce(extreme[:, HEADS:2 * HEADS], neg_as[:].rearrange("p b h -> p h b"), AX_X, ALU.max
                                        ).then_inc(s_ext, 1)
                dve.wait_ge(s_ar, l + 1)
                nc.vector.tensor_tensor(spread[:, 0:HEADS], extremes[:, 0:HEADS], extremes[:, HEADS:2 * HEADS], ALU.add).then_inc(s_lay, 1)
                nc.vector.tensor_scalar(spread[:, HEADS:HEADS + 1], extremes[:, 2 * HEADS:2 * HEADS + 1], SPREAD / COUNT, None,
                                        ALU.mult).then_inc(s_lay, 1)
                dve.wait_ge(s_lay, 6 * l + 4)
                nc.vector.tensor_reduce(spread[:, HEADS + 1:HEADS + 2], spread[:, 0:HEADS + 1], AX_X, ALU.max).then_inc(s_lay, 1)
                dve.wait_ge(s_lay, 6 * l + 5)
                nc.vector.tensor_scalar(route_f[:, 0:1], spread[0:1, HEADS + 1:HEADS + 2], SPREAD, None, ALU.is_gt).then_inc(s_lay, 1)
                dve.wait_ge(s_lay, 6 * l + 6)
                nc.vector.tensor_copy(route[:], route_f[:]).then_inc(s_route, 1)
                dve.wait_ge(s_route, l + 1)
                stand(dve)
                general = dve.value_load(route[0:1, 0:1], min_val=0, max_val=1)
                g = dve.value_load(route[0:1, 1:2], min_val=0, max_val=LAYERS)
                f = dve.value_load(route[0:1, 2:3], min_val=0, max_val=LAYERS)
                nc.vector.tensor_tensor(route_f[:, 1:2], route_f[:, 1:2], route_f[:, 0:1], ALU.add).then_inc(s_lay2, 1)
                nc.vector.scalar_tensor_tensor(route_f[:, 2:3], route_f[:, 2:3], 1.0, route_f[:, 0:1], ALU.add, ALU.subtract
                                               ).then_inc(s_lay2, 1)
                dve.wait_ge(s_lay2, 2 * l + 2)
                stand(dve)
                with dve.If(general == 1):
                    with dve.Fori(0, NFC) as c:
                        with dve.Fori(0, NB) as b:
                            m = g * STEPS + c * NB + b
                            dve.wait_ge(s_rpl, 16 * PLANES * (m + 1))
                            dve.wait_ge(s_rtr, m + 1)
                            nc.vector.tensor_tensor(r_pl[:, 0, :], r_pl[:, 0, :], r_pl[:, 1, :], ALU.add).then_inc(s_rop, 1)
                            nc.vector.tensor_tensor(r_pl[:, 2, :], r_pl[:, 2, :], r_pl[:, 3, :], ALU.add).then_inc(s_rop, 1)
                            dve.wait_ge(s_rop, 2 * m + 2)
                            nc.vector.tensor_tensor(r_cnt[:], r_pl[:, 0, :], r_pl[:, 2, :], ALU.add).then_inc(s_rsum, 1)
                    with dve.Fori(0, NCH) as c:
                        t = g * NCH + c
                        dve.wait_ge(s_amax, t + 1)
                        nc.vector.memset(run_max, -2.0 * BIG).then_inc(s_rm, 1)
                        with dve.Fori(0, NB // RING) as i:
                            for j in range(RING):
                                base = t * MAXOPS + 1 + (1 + HEADS) * (i * RING + j)
                                dve.wait_ge(s_c[j], 48 * (2 * t * (NB // RING) + i + 1))
                                dve.wait_ge(s_rm, base)
                                nc.vector.tensor_scalar(absent[:], c_in[:, j, :], 0.0, -BIG, ALU.is_equal, ALU.mult).then_inc(s_rm, 1)
                                dve.wait_ge(s_rm, base + 1)
                                for h in range(HEADS):
                                    r = run_max[:, h * CH:(h + 1) * CH]
                                    nc.vector.scalar_tensor_tensor(r, absent[:], as_in[:, j, h:h + 1], r, ALU.add, ALU.max
                                                                   ).then_inc(s_rm, 1)
                        dve.wait_ge(s_amax, t + 2)
                        dve.wait_ge(s_ad, t + 1)
                        nc.vector.tensor_tensor(heads_of(m_row), psS[:, :, 0:CH], heads_of(all_max), ALU.add).then_inc(s_m, 1)
                        dve.wait_ge(s_m, 4 * t + 1)
                        nc.vector.scalar_tensor_tensor(m_row, m_row, 0.2, m_row, ALU.mult, ALU.max).then_inc(s_m, 1)
                        nc.vector.tensor_scalar(all_max, all_max, -0.5 * BIG, None, ALU.is_gt).then_inc(s_m, 1)
                        dve.wait_ge(s_m, 4 * t + 3)
                        nc.vector.tensor_tensor(m_row, m_row, all_max, ALU.mult).then_inc(s_m, 1)
                        dve.wait_ge(s_m, 4 * t + 4)
                        stand(dve)
                        with dve.Fori(0, NB // RING) as i:
                            for j in range(RING):
                                n = t * NB + i * RING + j
                                w = g_wts[:, j, :]
                                dve.wait_ge(s_z, n + 1)
                                nc.vector.scalar_tensor_tensor(w, w, 0.2, w, ALU.mult, ALU.max).then_inc(s_zm, 1)
                                dve.wait_ge(s_zm, 2 * n + 1)
                                nc.vector.tensor_tensor(w, w, m_row, ALU.subtract).then_inc(s_zm, 1)
                                dve.wait_ge(s_ez, n + 1)
                                dve.wait_ge(s_c[j], 48 * (2 * t * (NB // RING) + NB // RING + i + 1))
                                nc.vector.scalar_tensor_tensor(heads_of(w), heads_of(w), 1.0,
                                                               c_in[:, j, :].unsqueeze(1).to_broadcast([P, HEADS, CH]),
                                                               ALU.min, ALU.mult).then_inc(s_gw, 1)
                        epilogue(t, 1e-16, (s_gpv, t * NB + NB + RING), g_num, g_den)
                        o = outT[:, bass.ds(c * CH, CH)]
                        nc.vector.tensor_tensor(g_num[:], g_num[:], g_den[:], ALU.mult).then_inc(s_ep, 1)
                        dve.wait_ge(s_ep, t * 3 + 3)
                        nc.vector.tensor_scalar(o, g_num[:], bias[:, 0:1], 0.0, ALU.add, ALU.max).then_inc(s_relu, 1)
                    dve.wait_ge(s_relu, (g + 1) * NCH)
                    nc.vector.tensor_copy(featT[:, 0:NC], outT[:, 0:NC]).then_inc(s_layer, 1)

                with dve.Else():
                    W = DH + 1
                    top = extremes[:, 0:HEADS].unsqueeze(1).to_broadcast([P, NB, HEADS])
                    own = [0]

                    def link_fast(ins):
                        own[0] += 1
                        ins.then_inc(s_own, 1)
                        dve.wait_ge(s_own, CHAINED * f + own[0])
                    nc.vector.tensor_tensor(neg_as[:], neg_as[:], top, ALU.add).then_inc(s_sc, 1)
                    link_fast(nc.vector.tensor_tensor(scale_d[:, 0], logit[:, :, HEADS:2 * HEADS], top, ALU.add))
                    link_fast(nc.vector.tensor_scalar(scale_d[:, 1], scale_d[:, 0], -0.8, 0.0, ALU.mult, ALU.min))
                    nc.vector.tensor_scalar(scale_d[:, 0], scale_d[:, 0], 0.8, 0.0, ALU.mult, ALU.min).then_inc(s_sc, 1)
                    dve.wait_ge(s_sce, 2 * f + 1)
                    halves = [slice(half * NB * HEADS // 2, (half + 1) * NB * HEADS // 2) for half in range(2)]
                    hv = h_sb[:].rearrange("p b (h c) -> p (b h) c", h=HEADS)[:, :, 0:W]
                    for half, a in enumerate(halves):
                        n_a = a.stop - a.start
                        nc.vector.tensor_tensor(terms[:, a, :].rearrange("p a (k f) -> p a k f", k=2),
                                                hv[:, a, :].unsqueeze(2).to_broadcast([P, n_a, 2, W]),
                                                scale_s[:].rearrange("p b h k -> p (b h) k")[:, a, :].unsqueeze(3)
                                                .to_broadcast([P, n_a, 2, W]), ALU.mult).then_inc(s_term, 1)
                    for k in range(2):
                        for half, a in enumerate(halves):
                            dve.wait_ge(s_part, 4 * f + 2 * k + half + 1)
                            o = terms[:, a, :] if k == 0 else parts[:, a, 2, :]
                            ins = nc.vector.tensor_tensor(o, terms[:, a, :], parts[:, a, k, :], ALU.subtract)
                            ins.then_inc(s_term if k == 0 else s_low, 1)
                    dve.wait_ge(s_sce, 2 * f + 2)
                    link_fast(nc.vector.tensor_scalar(neg_as[:], logit[:, :, 0:HEADS], -1.0, None, ALU.mult))
                    dve.wait_ge(s_adre, (l + 1) * (NR // AW) * HEADS + HEADS)
                    stand(dve)
                    with dve.Fori(0, NFC) as c:
                        with dve.Fori(0, NB // RING) as i:
                            for j in range(RING):
                                t = f * NFC + c
                                n = t * NB + i * RING + j
                                dve.wait_ge(s_fc[j], 16 * (t * (NB // RING) + i + 1))
                                for h in range(HEADS - 1):
                                    dve.wait_ge(s_head, HEADS * (n + RING) + h + 1 - UR)
                                    nc.vector.scalar_tensor_tensor(chosen[:, (j * HEADS + h) % UR, :],
                                                                   ad_row[:, h, bass.ds(c * FC, FC)],
                                                                   one(neg_as[:, bass.ds(i * RING + j, 1), h:h + 1]),
                                                                   c16[:, j, :], ALU.is_ge, ALU.mult).then_inc(s_chosen, 1)
                    dve.wait_ge(s_comb, 4 * (f + 1) * NFC + 1)
                    link_fast(nc.vector.tensor_scalar(rden[:], total[:, :, :, DH:W].rearrange("p b h o -> p b (h o)"), 1e-30, None, ALU.max))
                    link_fast(nc.vector.reciprocal(rden[:], rden[:]))
                    nc.vector.memset(x_next.rearrange("p b (h c) -> p (b h) c", h=HEADS)[:, :, DH:HS], 0.0)
                    nc.vector.tensor_tensor(wide(x_next), total[:, :, :, 0:DH],
                                            rden[:].unsqueeze(3).to_broadcast([P, NB, HEADS, DH]), ALU.mult).then_inc(s_xn, 1)
                    assert own[0] == CHAINED
                    dve.wait_ge(s_xte, (f + 1) * len(G4))
                    dve.sem_inc(s_layer, 1)

            for m, g, k in G4:
                dve.wait_ge(s_f, m + 1)
                nc.vector.tensor_tensor(narrow(y_sb[:, g:g + k, :]), wide(psP[:, m % 2, 0:k * P].rearrange("p (b f) -> p b f", b=k)),
                                        wide(x1[:, g:g + k, :]), ALU.add).then_inc(s_fe, 1)
            dve.wait_ge(s_fe, len(G4))
            layernorm(2, y_sb)
            nc.vector.tensor_tensor(y_sb, y_sb, stat[:, 3, :].unsqueeze(2).to_broadcast([P, NB, D]), ALU.mult).then_inc(s_fin, 1)


_INS = ["x", "src", "dst", "L0_gnn_qW", "L0_gnn_kW", "L0_gnn_vW", "L1_gnn_W", "L1_gnn_att_src", "L1_gnn_att_dst", "L1_gnn_bias"]


def kernel(**inputs):
    import numpy as _np
    import concourse.bacc as _bacc
    from concourse import mybir as _mybir
    from concourse.bass_utils import run_bass_kernel_spmd as _run

    nc = _bacc.Bacc("TRN2", target_bir_lowering=False, num_devices=1)
    arrays, args = {}, []
    for name in _INS:
        a = _np.ascontiguousarray(inputs[name])
        arrays[f"in_{name}_dram"] = a
        args.append(nc.dram_tensor(f"in_{name}_dram", a.shape, _mybir.dt.from_np(a.dtype), kind="ExternalInput").ap())
    x = inputs["x"]
    args.append(nc.dram_tensor("out_0_dram", x.shape, _mybir.dt.float32, kind="ExternalOutput").ap())
    build(nc, *args)
    r = _run(nc, [arrays], core_ids=[0])
    return r.results[0]["out_0_dram"]
```
